# Optimizing a Trainium2 kernel written in Bass

```python
import numpy as np
import jax
import jax.numpy as jnp

def _softmax(x, axis=-1):
    return jax.nn.softmax(x, axis=axis)

def _gelu(x):
    return jax.nn.gelu(x, approximate=True)

def _silu(x):
    return jax.nn.silu(x)

def _sigmoid(x):
    return jax.nn.sigmoid(x)

def _layernorm(x, axis=-1, eps=1e-05):
    m = jnp.mean(x, axis=axis, keepdims=True)
    v = jnp.var(x, axis=axis, keepdims=True)
    return (x - m) / jnp.sqrt(v + eps)

def _scatter_add(tgt, idx, src, axis=0):
    return tgt.at[idx].add(src)

def _segment_sum(src, seg, n):
    return jax.ops.segment_sum(src, seg, n)
kernel_name = 'mk_decoder_postln_d1_seqx_r4_9599a9'

def setup_inputs(seed: int=0):
    np.random.seed(seed)
    _w = jnp.asarray

    def _rec_inputs():
        import jax
        import jax.numpy as jnp
        _rk = jax.random.key(seed)
        x = -0.0002928 + 1 * jax.random.normal(jax.random.fold_in(_rk, 1), (32, 128, 256), jnp.float32)
        _lenS = 128 - jax.random.randint(jax.random.fold_in(_rk, 7), (32,), 0, max(1, 128 // 4) + 1, jnp.int32)
        _lenS2 = 128 - jax.random.randint(jax.random.fold_in(_rk, 8), (32,), 0, max(1, 128 // 4) + 1, jnp.int32)
        _ctx_1024P = jax.random.normal(jax.random.fold_in(_rk, 11), (32, 16, 256), jnp.float32)
        _ctx_1024c = jax.random.dirichlet(jax.random.fold_in(_rk, 511), 0.3 * jnp.ones((16,), jnp.float32), (32, 128))
        _ctx_1024t = jnp.einsum('bsk,bkd->bsd', _ctx_1024c, _ctx_1024P)
        _ctx_1024t = _ctx_1024t * jax.lax.rsqrt(jnp.mean(jnp.square(_ctx_1024t)) + 1e-12) * 0.953939
        ctx_1024 = -1.39393e-06 + 0.999914 * (_ctx_1024t + 0.3 * jax.random.normal(jax.random.fold_in(_rk, 611), (32, 128, 256), jnp.float32))
        _validS = jnp.arange(128)[None, :] < _lenS[:, None]
        _validS2 = jnp.arange(128)[None, :] < _lenS2[:, None]
        _causal = jnp.tril(jnp.ones((128, 128), dtype=bool))
        mask_1x1xSxS2_ik0 = jnp.where(jnp.broadcast_to(_validS2[0:1, None, None, :], (1, 1, 128, 128)), 0, 1).astype(jnp.int32)
        return (x, ctx_1024, mask_1x1xSxS2_ik0)
    x, ctx_1024, mask_1x1xSxS2_ik0 = _rec_inputs()

    def _L0_attn_setup():
        import jax, jax.numpy as jnp
        import numpy as np
        import math
        D_MODEL = 256
        N_HEAD = 16
        DH = D_MODEL // N_HEAD
        key = jax.random.key(seed)
        k1, k2, k3, k4, k5 = jax.random.split(key, 5)
        bs, seq = (2, 512)
        scale = 1.0 / math.sqrt(D_MODEL)
        return {'x': jax.random.normal(k1, (bs, seq, D_MODEL), dtype=jnp.float32), 'W_qkv': jax.random.normal(k2, (D_MODEL, 3 * D_MODEL), dtype=jnp.float32) * scale, 'b_qkv': jax.random.normal(k3, (3 * D_MODEL,), dtype=jnp.float32) * 0.02, 'W_proj': jax.random.normal(k4, (D_MODEL, D_MODEL), dtype=jnp.float32) * scale, 'b_proj': jax.random.normal(k5, (D_MODEL,), dtype=jnp.float32) * 0.02}
    _L0_attn_all = _L0_attn_setup()
    _L0_attn_in = {k: v for k, v in _L0_attn_all.items() if k in ('W_qkv', 'b_qkv', 'W_proj', 'b_proj')}
    del _L0_attn_all

    def _L0_xattn_setup():
        import jax, jax.numpy as jnp
        import numpy as np
        D_MODEL = 256
        H = 16
        D_K = D_MODEL // H
        NEG = -1000000000.0

        def _split_heads(x):
            B, S, _ = x.shape
            return x.reshape(B, S, H, D_K).transpose(0, 2, 1, 3)
        key = jax.random.key(seed)
        ks = jax.random.split(key, 12)
        B, S = (2, 512)
        s = 1.0 / np.sqrt(D_MODEL)
        inp = {'q': jax.random.normal(ks[0], (B, S, D_MODEL), jnp.float32), 'k': jax.random.normal(ks[1], (B, S, D_MODEL), jnp.float32), 'v': jax.random.normal(ks[2], (B, S, D_MODEL), jnp.float32), 'mask': jnp.tril(jnp.ones((S, S), jnp.int32))[None, None, :, :], 'wq': jax.random.normal(ks[3], (D_MODEL, D_MODEL), jnp.float32) * s, 'bq': jax.random.normal(ks[4], (D_MODEL,), jnp.float32) * s, 'wk': jax.random.normal(ks[5], (D_MODEL, D_MODEL), jnp.float32) * s, 'bk': jax.random.normal(ks[6], (D_MODEL,), jnp.float32) * s, 'wv': jax.random.normal(ks[7], (D_MODEL, D_MODEL), jnp.float32) * s, 'bv': jax.random.normal(ks[8], (D_MODEL,), jnp.float32) * s, 'wo': jax.random.normal(ks[9], (D_MODEL, D_MODEL), jnp.float32) * s, 'bo': jax.random.normal(ks[10], (D_MODEL,), jnp.float32) * s}
        return inp
    _L0_xattn_all = _L0_xattn_setup()
    _L0_xattn_in = {k: v for k, v in _L0_xattn_all.items() if k in ('wq', 'bq', 'wk', 'bk', 'wv', 'bv', 'wo', 'bo')}
    del _L0_xattn_all

    def _L0_ffn_setup():
        import jax, jax.numpy as jnp
        import numpy as np
        NUM_HEADS = 16
        TOP_K = 2
        key = jax.random.key(seed)
        ks = jax.random.split(key, 5)
        B, S, D, E = (4, 512, 256, 8)
        scale = 0.02
        return {'x': jax.random.normal(ks[0], (B, S, D), dtype=jnp.float32), 'W_qkv': jax.random.normal(ks[1], (D, 3 * D), dtype=jnp.float32) * scale, 'b_qkv': jnp.zeros((3 * D,), dtype=jnp.float32), 'W_gate': jax.random.normal(ks[2], (D, E), dtype=jnp.float32) * scale, 'b_gate': jnp.zeros((E,), dtype=jnp.float32), 'W_experts': jax.random.normal(ks[3], (E, D, D), dtype=jnp.float32) * scale, 'b_experts': jnp.zeros((E, D), dtype=jnp.float32)}
    _L0_ffn_all = _L0_ffn_setup()
    _L0_ffn_in = {k: v for k, v in _L0_ffn_all.items() if k in ('W_qkv', 'b_qkv', 'W_gate', 'b_gate', 'W_experts', 'b_experts')}
    del _L0_ffn_all
    return {'x': x, 'ctx_1024': ctx_1024, 'mask_1x1xSxS2_ik0': mask_1x1xSxS2_ik0, 'L0_attn_W_qkv': _L0_attn_in['W_qkv'], 'L0_attn_b_qkv': _L0_attn_in['b_qkv'], 'L0_attn_W_proj': _L0_attn_in['W_proj'], 'L0_attn_b_proj': _L0_attn_in['b_proj'], 'L0_xattn_wq': _L0_xattn_in['wq'], 'L0_xattn_bq': _L0_xattn_in['bq'], 'L0_xattn_wk': _L0_xattn_in['wk'], 'L0_xattn_bk': _L0_xattn_in['bk'], 'L0_xattn_wv': _L0_xattn_in['wv'], 'L0_xattn_bv': _L0_xattn_in['bv'], 'L0_xattn_wo': _L0_xattn_in['wo'], 'L0_xattn_bo': _L0_xattn_in['bo'], 'L0_ffn_W_qkv': _L0_ffn_in['W_qkv'], 'L0_ffn_b_qkv': _L0_ffn_in['b_qkv'], 'L0_ffn_W_gate': _L0_ffn_in['W_gate'], 'L0_ffn_b_gate': _L0_ffn_in['b_gate'], 'L0_ffn_W_experts': _L0_ffn_in['W_experts'], 'L0_ffn_b_experts': _L0_ffn_in['b_experts']}

def reference(x, ctx_1024, mask_1x1xSxS2_ik0, L0_attn_W_qkv, L0_attn_b_qkv, L0_attn_W_proj, L0_attn_b_proj, L0_xattn_wq, L0_xattn_bq, L0_xattn_wk, L0_xattn_bk, L0_xattn_wv, L0_xattn_bv, L0_xattn_wo, L0_xattn_bo, L0_ffn_W_qkv, L0_ffn_b_qkv, L0_ffn_W_gate, L0_ffn_b_gate, L0_ffn_W_experts, L0_ffn_b_experts):
    import jax
    import jax.numpy as jnp

    def _L0_attn_ref(x, W_qkv, b_qkv, W_proj, b_proj):
        import jax, jax.numpy as jnp
        import numpy as np
        import math
        D_MODEL = 256
        N_HEAD = 16
        DH = D_MODEL // N_HEAD
        bs, seq, _ = x.shape
        qkv = x @ W_qkv + b_qkv
        q, k, v = jnp.split(qkv, 3, axis=-1)
        q = q.reshape(bs, seq, N_HEAD, DH).transpose(0, 2, 1, 3)
        k = k.reshape(bs, seq, N_HEAD, DH).transpose(0, 2, 1, 3)
        v = v.reshape(bs, seq, N_HEAD, DH).transpose(0, 2, 1, 3)
        attn = jnp.einsum('bhqd,bhkd->bhqk', q, k) * (1.0 / math.sqrt(DH))
        causal = jnp.tril(jnp.ones((seq, seq), dtype=bool))
        attn = jnp.where(causal, attn, -jnp.inf)
        attn = jax.nn.softmax(attn, axis=-1)
        z = jnp.einsum('bhqk,bhkd->bhqd', attn, v)
        z = z.transpose(0, 2, 1, 3).reshape(bs, seq, D_MODEL)
        return z @ W_proj + b_proj

    def _L0_xattn_ref(q, k, v, mask, wq, bq, wk, bk, wv, bv, wo, bo):
        import jax, jax.numpy as jnp
        import numpy as np
        D_MODEL = 256
        H = 16
        D_K = D_MODEL // H
        NEG = -1000000000.0

        def _split_heads(x):
            B, S, _ = x.shape
            return x.reshape(B, S, H, D_K).transpose(0, 2, 1, 3)
        query = _split_heads(q @ wq.T + bq)
        key = _split_heads(k @ wk.T + bk)
        value = _split_heads(v @ wv.T + bv)
        scores = jnp.einsum('bhqd,bhkd->bhqk', query, key) / jnp.sqrt(jnp.asarray(D_K, query.dtype))
        scores = jnp.where(mask == 0, jnp.asarray(NEG, scores.dtype), scores)
        attn = jax.nn.softmax(scores, axis=-1)
        x = jnp.einsum('bhqk,bhkd->bhqd', attn, value)
        B, _, S, _ = x.shape
        x = x.transpose(0, 2, 1, 3).reshape(B, S, D_MODEL)
        return x @ wo.T + bo

    def _L0_ffn_ref(x, W_qkv, b_qkv, W_gate, b_gate, W_experts, b_experts):
        import jax, jax.numpy as jnp
        import numpy as np
        NUM_HEADS = 16
        TOP_K = 2
        B, S, D = x.shape
        H = NUM_HEADS
        hd = D // H
        E = W_gate.shape[-1]
        qkv = (x @ W_qkv + b_qkv).reshape(B, S, 3, H, hd)
        q, k, v = (qkv[:, :, 0], qkv[:, :, 1], qkv[:, :, 2])
        attn = jnp.einsum('bqhd,bkhd->bhqk', q, k) / jnp.sqrt(jnp.asarray(hd, x.dtype))
        attn = jax.nn.softmax(attn, axis=-1)
        attn_out = jnp.einsum('bhqk,bkhd->bqhd', attn, v).reshape(B, S, D)
        gate = jax.nn.softmax(x @ W_gate + b_gate, axis=-1)
        top_g, top_i = jax.lax.top_k(gate, TOP_K)
        combine = jnp.sum(jax.nn.one_hot(top_i, E, dtype=x.dtype) * top_g[..., None], axis=2)
        expert_out = jnp.einsum('bsd,edf->bsef', x, W_experts) + b_experts
        moe_out = jnp.einsum('bsef,bse->bsf', expert_out, combine)
        return attn_out + moe_out
    x = _layernorm(x + _L0_attn_ref(x, L0_attn_W_qkv, L0_attn_b_qkv, L0_attn_W_proj, L0_attn_b_proj), axis=-1)
    x = _layernorm(x + _L0_xattn_ref(x, ctx_1024, ctx_1024, mask_1x1xSxS2_ik0, L0_xattn_wq, L0_xattn_bq, L0_xattn_wk, L0_xattn_bk, L0_xattn_wv, L0_xattn_bv, L0_xattn_wo, L0_xattn_bo), axis=-1)
    x = _layernorm(x + _L0_ffn_ref(x, L0_ffn_W_qkv, L0_ffn_b_qkv, L0_ffn_W_gate, L0_ffn_b_gate, L0_ffn_W_experts, L0_ffn_b_experts), axis=-1)
    return x

_drawn_inputs = setup_inputs


def setup_inputs(seed=0):
    import zlib

    import numpy as np

    out = dict(_drawn_inputs(seed))
    spreads = {'L0_ffn_b_qkv': (0.0, 0.1), 'L0_ffn_b_gate': (0.0, 0.1), 'L0_ffn_b_experts': (0.0, 0.331)}
    factors = {'L0_attn_b_proj': 2.951}
    for name, (base, spread) in spreads.items():
        noise = np.random.default_rng([zlib.crc32(name.encode()), seed]).standard_normal(out[name].shape)
        drawn = base * np.exp(spread * noise) if base else spread * noise
        out[name] = jnp.asarray(drawn.astype(out[name].dtype))
    for name, factor in factors.items():
        out[name] = (out[name] * factor).astype(out[name].dtype)
    return out
```

```python
from contextlib import ExitStack

import concourse.bass as bass
from concourse import mybir
from concourse.alu_op_type import AluOpType as ALU

ACT = mybir.ActivationFunctionType
F32 = mybir.dt.float32
F32R = mybir.dt.float32r
BF16 = mybir.dt.bfloat16
U32 = mybir.dt.uint32
AX = mybir.AxisListType

P = 128
D = 256
H = 16
DH = D // H
E = 8
B = 32
PB = 2
TOK = PB * P
NSTEP = B // PB
NL = 3
C = D // P
QUAD = 32
SCALE = DH ** -0.5
EPS = 1e-5
MASKED = -(2.0 ** 100)
VG = D + E

WQ, WK, WV, WO = 0, D, 2 * D, 3 * D
WE = 2 * D + VG
WCOLS = [4 * D, 4 * D, WE + E * D]
RB_V = [0, 2 * D, 4 * D]
RB_O = [D, 3 * D]
RB_COLS = 4 * D + VG

PAIRS = H // 2
STEP_TICKS = 24
LAYER_START = [7.35, 39.35, 71.35]
ATTENTION_TIMES = (
    [(0.0, "xt", 0), (1.0, "q", 0), (1.6, "k", 0), (2.2, "v", 0)]
    + [(4.0 + p / 2, "max", p) for p in range(PAIRS)] + [(8.3, "maxt", 0)]
    + [(8.7 + 0.97 * p, "attend", p) for p in range(PAIRS + 1)] + [(14.6, "z", 0), (17.4, "z", 1)]
)
OUTPUT_TIMES = [(18.4, "zt", 0), (19.4, "out", 0)]
EXPERT_TIMES = (
    [(5.6, "gate", 0), (6.1, "bias", 0)]
    + [(t, "experts", g) for g, t in enumerate((6.2, 7.5, 13.0, 14.2, 15.4, 19.5, 21.0, 22.5))]
    + [(23.8, "finish", 0)]
)
LAYER_TIMES = [ATTENTION_TIMES + OUTPUT_TIMES, ATTENTION_TIMES + [(0.4, "ct", 0)] + OUTPUT_TIMES,
               ATTENTION_TIMES + EXPERT_TIMES]
TIMETABLE = sorted(((LAYER_START[l] + t) % STEP_TICKS, l, kind, int((LAYER_START[l] + t) // STEP_TICKS), part)
                   for l in range(NL) for t, kind, part in LAYER_TIMES[l])
UNITS = [(kind, l, lag, part) for _, l, kind, lag, part in TIMETABLE]
DEPTH = max(u[2] for u in UNITS)
PROJ_ORDER = [u[1:3] for u in UNITS if u[0] == "q"]
MAX_ORDER = [u[1:3] for u in UNITS if u[0] == "max" and u[3] == 0]
ATT_ORDER = [u[1:3] for u in UNITS if u[0] == "attend" and u[3] == 0]
HALF = [0, 1, 0]
WORK_BANKS = 4


def work_uses():
    uses = []
    for kind, l, lag, part in UNITS:
        if kind in ("xt", "ct", "q", "k", "v", "maxt", "gate", "bias", "zt", "out"):
            uses.append((kind, l, lag))
        if kind == "v" and l == 2:
            uses.append(("v1", l, lag))
        if kind == "attend" and part in (1, 5):
            uses.append((f"pv{part // 4}", l, lag))
        if kind == "z":
            uses.append((f"z{part}", l, lag))
        if kind == "experts":
            uses.append((f"e{part}", 2, lag))
    return uses


USES = work_uses()
BANK_OF = {}
for _use in USES:
    BANK_OF[_use[:2]] = 0 if _use[0].startswith("pv") else 1 + sum(v > 0 for v in BANK_OF.values()) % (WORK_BANKS - 1)
assert len(BANK_OF) == len(USES)


def active(i, lag):
    return i is None or 0 <= i - lag < NSTEP


def decoder(nc, x, ctx, mask, w, rows, cols, eb, consts, out):
    with ExitStack() as stack:
        def sb(name, shape, dt=F32):
            return stack.enter_context(nc.sbuf_tensor(name, shape, dt))

        def sem(name):
            return stack.enter_context(nc.semaphore(name))

        def per_layer(name, layers=range(NL)):
            return {l: sem(f"{name}_{l}") for l in layers}

        def bufs(name, shape, dt=F32, n=NL):
            return [sb(f"{name}{l}", shape, dt) for l in range(n)]

        X = bufs("x", [P, PB, D])
        XB = bufs("res", [P, PB, D])
        CTX = sb("ctx", [P, PB, D])
        XH = bufs("x_hi", [P, C, TOK], F32R)
        XL = bufs("x_lo", [P, C, TOK], F32R)
        CH = sb("c_hi", [P, C, TOK], F32R)
        CL = sb("c_lo", [P, C, TOK], F32R)
        QF = sb("q_full", [P, C, TOK])
        KF = sb("k_full", [P, C, TOK])
        QH = bufs("q_hi", [P, C, TOK], F32R, 2)
        KH = bufs("k_hi", [P, C, TOK], F32R)
        KL = bufs("k_lo", [P, C, TOK], F32R)
        QBH = bufs("q_pair_hi", [P, C, 2, TOK], F32R)
        QBL = bufs("q_pair_lo", [P, C, 2, TOK], F32R)
        KBH = bufs("k_pair_hi", [P, C, 2, TOK], F32R, 2)
        VA = bufs("v_ones", [P, PB, H, QUAD])
        NM = sb("neg_max", [P, PB, H])
        NMB = sb("neg_max_parts", [P, PB, 4, 2, H], BF16)
        MT = bufs("neg_max_t", [P, TOK], BF16)
        PR = bufs("probs", [P, PB, 2, P], F32, 3)
        ZA = bufs("z_aug", [P, 4, P], F32, 2)
        Z = bufs("z", [P, PB, H, DH])
        RZ = sb("z_recip", [P, PB, PAIRS, 2])
        ST = sb("bn_stats", [P, NL, PB, 6])
        MV = sb("mean_var", [P, NL, PB, 2])
        VE = sb("var_eps", [P, NL, PB])
        RS = sb("rstd", [P, NL, PB])
        GL = sb("gate_logits", [P, PB, E])
        GN = sb("gate_neg_max", [P, PB])
        GE = sb("gate_exp", [P, PB, E])
        GS = sb("gate_sum", [P, PB])
        GR = sb("gate_recip", [P, PB])
        GP = sb("gate_probs", [P, PB, E])
        GT = sb("gate_top", [P, PB, 8])
        GI = sb("gate_index", [P, PB, 8], U32)
        GF = sb("gate_index_f", [P, PB, 8])
        G1 = sb("combine_first", [P, PB, E])
        G2 = sb("combine_second", [P, PB, E])
        CB = sb("combine", [P, PB, QUAD])
        CBT = sb("combine_t", [QUAD, TOK])
        WH = [sb(f"w_hi{l}", [P, C, WCOLS[l]], F32R) for l in range(NL)]
        WL = [sb(f"w_lo{l}", [P, C, WCOLS[l]], F32R) for l in range(NL)]
        IDF = sb("ident_f", [P, P])
        IDB = sb("ident_b", [P, P], BF16)
        CONST = sb("consts", [P, P + P + H + 2 + E])
        MI = sb("mask_int", [P, P], mybir.dt.int32)
        MF = sb("mask_f", [P, P])
        MQ = bufs("mask_qk", [P, P], BF16, 2)
        MK = bufs("mask_kq", [P, P], BF16, 2)
        SEL = sb("head_rows", [P, H, P], BF16)
        RB = sb("row_bias", [P, RB_COLS])
        COLB = sb("col_bias", [P, NL, 2, C])
        QBI = sb("q_bias_scaled", [P, NL, C])
        EB = sb("expert_bias", [E, D])
        NHALF = sb("minus_half", [P, PB])
        EPSC = sb("epsilon", [P, PB])
        SPARE = sb("spare", [P, 1])

        SM = [stack.enter_context(nc.psum_tensor(f"max_scores{i}", [P, PB, 2, P], F32)) for i in range(2)]
        SS = [stack.enter_context(nc.psum_tensor(f"scores{i}", [P, PB, 2, P], F32)) for i in range(2)]
        WB = [stack.enter_context(nc.psum_tensor(f"work{i}", [P, 512], F32)) for i in range(WORK_BANKS)]

        def bank(name, l):
            return WB[BANK_OF[(name, l)]]

        const_loaded = sem("const_loaded")
        stage_loaded = [sem(f"stage_loaded{n}") for n in range(3)]
        w_hi_done = sem("w_hi_done")
        w_lo_done = sem("w_lo_done")
        setup_v = sem("setup_v")
        setup_pe = sem("setup_pe")
        setup_p = sem("setup_p")
        dve_setup = sem("dve_setup")
        x_loaded = sem("x_loaded")
        ctx_loaded = sem("ctx_loaded")
        out_stored = sem("out_stored")
        xt_psum = per_layer("xt_psum")
        xh_done = per_layer("xh_done")
        xl_done = per_layer("xl_done")
        xb_done = per_layer("xb_done", (0, 1))
        ct_psum, ch_done, cl_done = sem("ct_psum"), sem("ch_done"), sem("cl_done")
        q_psum = per_layer("q_psum")
        k_psum = per_layer("k_psum")
        v_psum = {(l, b): sem(f"v_psum_{l}{b}") for l, b in ((0, 0), (1, 0), (2, 0), (2, 1))}
        v_done = {(l, b): sem(f"v_done_{l}{b}") for l, b in ((0, 0), (1, 0), (2, 0), (2, 1))}
        qf_done = per_layer("qf_done")
        qbh_done = per_layer("qbh_done")
        kf_done = per_layer("kf_done")
        qh_done = per_layer("qh_done")
        kh_done = per_layer("kh_done")
        qb_done = per_layer("qb_done")
        kb_done = per_layer("kb_done")
        nm_done = per_layer("nm_done")
        mt_psum = per_layer("mt_psum")
        mt_done = per_layer("mt_done")
        za_done = {(l, f): sem(f"za_done_{l}{f}") for l in range(NL) for f in range(2)}
        z_psum = {(l, f): sem(f"z_psum_{l}{f}") for l in range(NL) for f in range(2)}
        z_done = {(l, f): sem(f"z_done_{l}{f}") for l in range(NL) for f in range(2)}
        zt_psum = per_layer("zt_psum", (0, 1))
        zh_done = per_layer("zh_done", (0, 1))
        zl_done = per_layer("zl_done", (0, 1))
        o_psum = per_layer("o_psum", (0, 1))
        sum_done = per_layer("sum_done")
        mv_done = per_layer("mv_done")
        ve_done = per_layer("ve_done")
        rs_done = per_layer("rs_done")
        norm_done = per_layer("norm_done")
        max_psum = sem("max_psum")
        max_read = sem("max_read")
        score_psum = sem("score_psum")
        probs_done = sem("probs_done")
        pv_psum = sem("pv_psum")
        vector_link = sem("vector_link")
        gate_max, gate_exp, combine_done = sem("gate_max"), sem("gate_exp"), sem("combine_done")
        gt_psum, gt_done, eb_psum, eb_done = sem("gt_psum"), sem("gt_done"), sem("eb_psum"), sem("eb_done")
        e_psum = [sem(f"e_psum_{g}") for g in range(E)]
        e_half = [sem(f"e_half_{g}") for g in range(E)]

        e_done = [sem(f"e_done_{g}") for g in range(E)]

        read_by = {}
        for l in range(NL):
            read_by[("xt", l)] = xl_done[l]
            read_by[("q", l)] = qf_done[l]
            read_by[("k", l)] = kf_done[l]
            read_by[("v", l)] = v_done[(l, 0)]
            read_by[("maxt", l)] = mt_done[l]
            for f in range(2):
                read_by[(f"pv{f}", l)] = za_done[(l, f)]
                read_by[(f"z{f}", l)] = z_done[(l, f)]
        for l in (0, 1):
            read_by[("zt", l)] = zl_done[l]
            read_by[("out", l)] = sum_done[l]
        read_by[("ct", 1)] = cl_done
        read_by[("v1", 2)] = v_done[(2, 1)]
        read_by[("gate", 2)] = gt_done
        read_by[("bias", 2)] = eb_done
        for g in range(E):
            read_by[(f"e{g}", 2)] = e_done[g]

        def steps(eng, body):
            def straight(i):
                body({c: i + c for c in range(-DEPTH, 2)}, i, ring_base(MAX_ORDER, i), ring_base(ATT_ORDER, i))
            full = DEPTH + 1
            for i in range(full):
                straight(i)
            with eng.Fori(full, NSTEP) as i:
                at = {c: eng.snap(i + c) for c in range(-DEPTH, 2)}
                per = NL * PAIRS
                body(at, None, eng.snap(i * per - (per * full - ring_base(MAX_ORDER, full))),
                     eng.snap(i * per - (per * full - ring_base(ATT_ORDER, full))))
            for i in range(NSTEP, NSTEP + DEPTH):
                straight(i)

        def ring_base(order, i):
            return PAIRS * sum(active(j, lag) for j in range(i) for _, lag in order)

        def links(kind, l, part):
            return {"z": 1, "out": 1, "finish": 1}.get(kind, 0) + (kind == "max") * ((part == PAIRS - 1) + 6 * (l == 2 and part == 1))

        def link_base(i):
            return sum(links(kind, l, part) for j in range(i) for kind, l, lag, part in UNITS if active(j, lag))

        def turn(order, l, p, i):
            return PAIRS * [m for m, lag in order if active(i, lag)].index(l) + p

        def slot(order, l, p, i, n):
            return (ring_base(order, DEPTH + 1 if i is None else i) + turn(order, l, p, i)) % n

        def before(order, l, at, i):
            n = [m for m, _ in order].index(l)
            for m, lag in reversed(order[:n]):
                if active(i, lag):
                    return m, at[1 - lag]
            for m, lag in reversed(order):
                if active(i if i is None else i - 1, lag):
                    return m, at[-lag]
            return None, None

        def claim(eng, name, l, at, i):
            mine, uses = BANK_OF[(name, l)], [u[:2] for u in USES]
            here = uses.index((name, l))
            for use in reversed(USES[:here]):
                if BANK_OF[use[:2]] == mine and active(i, use[2]):
                    return eng.wait_ge(read_by[use[:2]], at[1 - use[2]])
            for use in reversed(USES):
                if BANK_OF[use[:2]] == mine and active(i if i is None else i - 1, use[2]):
                    return eng.wait_ge(read_by[use[:2]], at[-use[2]])

        x_v = x.rearrange("(n b) s d -> n s b d", b=PB)
        ctx_v = ctx.rearrange("(n b) s d -> n s b d", b=PB)
        out_v = out.rearrange("(n b) s d -> n s b d", b=PB)

        def cols_of(ap, a, b):
            return ap.rearrange("(c p) n -> p c n", p=P)[:, :, a:b]

        pieces = [
            (0, WQ, 2 * D, [(0, cols_of(w["qkv0"], 0, 2 * D))]),
            (0, WV, 2 * D, [(0, cols_of(w["qkv0"], 2 * D, 3 * D)), (D, cols_of(w["o0"], 0, D))]),
            (1, WQ, 2 * D, [(0, cols_of(w["q1"], 0, D)), (D, cols_of(w["k1"], 0, D))]),
            (1, WV, 2 * D, [(0, cols_of(w["v1"], 0, D)), (D, cols_of(w["o1"], 0, D))]),
            (2, WQ, 2 * D, [(0, cols_of(w["qkv2"], 0, 2 * D))]),
            (2, WV, VG, [(0, cols_of(w["qkv2"], 2 * D, 3 * D)), (D, cols_of(w["gate"], 0, E))]),
        ]
        for g in range(E // 2):
            pieces.append((2, WE + 2 * g * D, 2 * D,
                           [(j * D, cols_of(w["experts"][2 * g + j], 0, D)) for j in range(2)]))
        staged = [16 * sum(len(q[3]) for q in pieces[n % 3:n + 1:3]) for n in range(len(pieces))]

        def stage(n, ncols):
            return VA[n % 3][:, :, :, :].rearrange("p b h d -> p (b h d)")[:, 0:C * ncols].rearrange(
                "p (c n) -> p c n", c=C)

        block = stack.enter_context(nc.Block())

        @block.sync
        def _(sp):
            n_const = 0
            for dst, src in ((CONST[:, :], consts), (MI[:, :], mask), (RB[:, :], rows),
                             (COLB[:, :, :, :].rearrange("p l q c -> p (l q c)"), cols),
                             (EB[:, :], eb)):
                sp.dma_start(dst, src).then_inc(const_loaded, 16)
                n_const += 16
            sp.dma_start(X[0][:, :, :], x_v[0]).then_inc(x_loaded, 16)
            sp.dma_start(CTX[:, :, :], ctx_v[0]).then_inc(ctx_loaded, 16)
            for n, (l, c0, ncols, parts) in enumerate(pieces):
                if n >= 3:
                    sp.wait_ge(w_lo_done, n - 2)
                for off, src in parts:
                    sp.dma_start(stage(n, ncols)[:, :, off:off + src.shape[2]], src).then_inc(stage_loaded[n % 3], 16)

            def load_x(i, at1):
                sp.wait_ge(xt_psum[0], at1)
                sp.wait_ge(xb_done[0], at1)
                sp.dma_start(X[0][:, :, :], x_v[at1]).then_inc(x_loaded, 16)

            def load_ctx(i, at0):
                sp.wait_ge(ct_psum, at0)
                sp.dma_start(CTX[:, :, :], ctx_v[at0]).then_inc(ctx_loaded, 16)

            def store(n, at):
                sp.wait_ge(norm_done[2], at)
                sp.dma_start(out_v[n], XB[2][:, :, :]).then_inc(out_stored, 16)

            load_x(0, 1)
            load_x(1, 2)
            load_ctx(1, 1)
            with sp.Fori(2, NSTEP - 1) as i:
                one = sp.snap(i + 1)
                two = sp.snap(i - 1)
                load_x(i, one)
                load_ctx(i, sp.snap(i + 0))
                store(sp.snap(i - 2), two)
            load_ctx(NSTEP - 1, NSTEP - 1)
            for n in range(NSTEP - 3, NSTEP):
                store(n, n + 1)
            sp.wait_ge(out_stored, 16 * NSTEP)
            sp.wait_ge(const_loaded, n_const)

        CONSTS_LOADED = 16 * 5

        @block.tensor
        def _(pe):
            pe.wait_ge(setup_v, 1)
            for j in range(2):
                pe.transpose(WB[j][:, 0:P // 2].bitcast(BF16), MQ[j][:, :], IDB[:, :]).then_inc(setup_pe, 1)
            pe.wait_ge(setup_v, 3)
            pe.wait_ge(setup_p, 1)
            pe.wait_ge(w_lo_done, len(pieces))

            def three_pass(dst, lhs_h, lhs_l, rhs_h, rhs_l):
                for c in range(C):
                    mm = None
                    for k, (a, b) in enumerate(((lhs_h, rhs_h), (lhs_h, rhs_l), (lhs_l, rhs_h))):
                        mm = pe.matmul(dst, a(c), b(c), start=(c == 0 and k == 0), stop=(c == C - 1 and k == 2))
                return mm

            def transpose_tokens(src, dst):
                for b in range(PB):
                    for c in range(C):
                        mm = pe.transpose(dst[:, c * TOK + b * P:c * TOK + (b + 1) * P],
                                          src[:, b, c * P:(c + 1) * P], IDF[:, :])
                return mm

            def step(at, i, max_base, att_base):
                def mine(name, l):
                    claim(pe, name, l, at, i)
                    return bank(name, l)

                def xt(l, new, part):
                    if l == 0:
                        pe.wait_ge(x_loaded, new * 16)
                    else:
                        pe.wait_ge(norm_done[l - 1], new)
                    transpose_tokens(X[l], mine("xt", l)).then_inc(xt_psum[l], 1)

                def ct(l, new, part):
                    pe.wait_ge(ctx_loaded, new * 16)
                    transpose_tokens(CTX, mine("ct", 1)).then_inc(ct_psum, 1)

                def feature_major(name, l, off, hi, lo, done):
                    dst = mine(name, l)
                    for t in range(C):
                        mm = three_pass(dst[:, t * TOK:(t + 1) * TOK],
                                        lambda c: WH[l][:, c, off + t * P:off + (t + 1) * P],
                                        lambda c: WL[l][:, c, off + t * P:off + (t + 1) * P],
                                        lambda c: hi[:, c, :], lambda c: lo[:, c, :])
                    mm.then_inc(done, 1)

                def q(l, new, part):
                    pe.wait_ge(xl_done[l], new)
                    feature_major("q", l, WQ, XH[l], XL[l], q_psum[l])

                def source(l):
                    return (CH, CL) if l == 1 else (XH[l], XL[l])

                def k(l, new, part):
                    if l == 1:
                        pe.wait_ge(cl_done, new)
                    feature_major("k", l, WK, *source(l), k_psum[l])

                def v(l, new, part):
                    hi, lo = source(l)
                    width = VG if l == 2 else D
                    for b in range(PB):
                        if l == 2:
                            dst, done = mine(("v", "v1")[b], l)[:, 0:width], v_psum[(l, b)]
                        else:
                            dst, done = (mine("v", l) if b == 0 else bank("v", l))[:, b * D:(b + 1) * D], v_psum[(l, 0)]
                        mm = three_pass(dst, lambda c: hi[:, c, b * P:(b + 1) * P], lambda c: lo[:, c, b * P:(b + 1) * P],
                                        lambda c: WH[l][:, c, WV:WV + width], lambda c: WL[l][:, c, WV:WV + width])
                        if l == 2 or b == 1:
                            mm.then_inc(done, 1)

                def row_max(l, new, p):
                    if p == 0:
                        pe.wait_ge(qh_done[l], new)
                        pe.wait_ge(kb_done[l], new)
                    g = turn(MAX_ORDER, l, p, i)
                    if i != 0 or g >= 2:
                        pe.wait_ge(max_read, max_base + (g - 1))
                    dst = SM[g % 2]
                    j, t = QUAD * (p % 4), p // 4
                    for b in range(PB):
                        mm = pe.matmul(dst[:, b, :, :], QH[HALF[l]][j:j + QUAD, t, b * P:(b + 1) * P],
                                       KBH[HALF[l]][j:j + QUAD, t, :, b * P:(b + 1) * P],
                                       start=(b == 0), stop=(b == PB - 1 and l == 2),
                                       tile_position=(j, 0), skip_group_check=True)
                    if l < 2:
                        mm = pe.matmul(dst[:, :, :, :], IDB[:, :],
                                       MQ[l][:, :].unsqueeze(1).to_broadcast([P, 2 * PB, P]),
                                       start=False, stop=True, skip_group_check=True)
                    mm.then_inc(max_psum, 1)

                def max_t(l, new, part):
                    pe.wait_ge(nm_done[l], new)
                    dst = mine("maxt", l)
                    for b in range(PB):
                        mm = pe.transpose(dst[:, b * P // 2:(b + 1) * P // 2].bitcast(BF16),
                                          NMB[:, b, :, :, :].rearrange("p r k h -> p (r k h)"), IDB[:, :])
                    mm.then_inc(mt_psum[l], 1)

                def scores(l, p):
                    g = turn(ATT_ORDER, l, p, i)
                    if i != 0 or g >= 2:
                        pe.wait_ge(probs_done, att_base + (g - 1))
                    dst = SS[g % 2]
                    j, t = QUAD * (p % 4), p // 4
                    for b in range(PB):
                        tok = slice(b * P, (b + 1) * P)
                        for n, (kk, qq) in enumerate(((KH[l], QBH[l]), (KH[l], QBL[l]), (KL[l], QBH[l]))):
                            pe.matmul(dst[:, b, :, :], kk[j:j + QUAD, t, tok], qq[j:j + QUAD, t, :, tok],
                                      start=(b == 0 and n == 0), stop=False,
                                      tile_position=(j, 0), skip_group_check=True)
                    if l < 2:
                        pe.matmul(dst[:, :, :, :], IDB[:, :],
                                  MK[l][:, :].unsqueeze(1).to_broadcast([P, 2 * PB, P]),
                                  start=False, stop=False, skip_group_check=True)
                    for h2 in range(2):
                        mm = pe.matmul(dst[:, :, h2, :], SEL[j:j + QUAD, 2 * p + h2, :],
                                       MT[l][j:j + QUAD, :].rearrange("p (b q) -> p b q", b=PB),
                                       start=False, stop=(h2 == 1), tile_position=(j, 0), skip_group_check=True)
                    mm.then_inc(score_psum, 1)

                def values(l, p):
                    g = turn(ATT_ORDER, l, p, i)
                    dst = mine(f"pv{p // 4}", l) if p % 4 == 0 else bank(f"pv{p // 4}", l)
                    pe.wait_ge(probs_done, att_base + (g + 1))
                    for b in range(PB):
                        for h2 in range(2):
                            j = QUAD * (2 * b + h2)
                            mm = pe.matmul(dst[j:j + QUAD, (p % 4) * P:(p % 4 + 1) * P], VA[l][:, b, 2 * p + h2, :],
                                           PR[slot(ATT_ORDER, l, p, i, 3)][:, b, h2, :],
                                           start=True, stop=True, tile_position=(0, j))
                    mm.then_inc(pv_psum, 1)

                def attend(l, new, p):
                    if p == 0:
                        pe.wait_ge(mt_done[l], new)
                        pe.wait_ge(qb_done[l], new)
                        for b in range(PB if l == 2 else 1):
                            pe.wait_ge(v_done[(l, b)], new)
                    if p < PAIRS:
                        scores(l, p)
                    if p > 0:
                        values(l, p - 1)

                def z_tokens(l, new, f):
                    pe.wait_ge(za_done[(l, f)], new)
                    dst = mine(f"z{f}", l)
                    for p in range(4):
                        mm = pe.transpose(dst[:, p * P:(p + 1) * P], ZA[f][:, p, :], IDF[:, :])
                    mm.then_inc(z_psum[(l, f)], 1)

                def z_transposed(l, new, part):
                    for f in range(2):
                        pe.wait_ge(z_done[(l, f)], new)
                    transpose_tokens(Z[l][:, :, :, :].rearrange("p b h d -> p b (h d)"),
                                     mine("zt", l)).then_inc(zt_psum[l], 1)

                def out_proj(l, new, part):
                    pe.wait_ge(zl_done[l], new)
                    dst = mine("out", l)
                    for b in range(PB):
                        mm = three_pass(dst[:, b * D:(b + 1) * D],
                                        lambda c: XH[l][:, c, b * P:(b + 1) * P],
                                        lambda c: XL[l][:, c, b * P:(b + 1) * P],
                                        lambda c: WH[l][:, c, WO:WO + D], lambda c: WL[l][:, c, WO:WO + D])
                    mm.then_inc(o_psum[l], 1)

                def gate_t(l, new, part):
                    pe.wait_ge(combine_done, new)
                    dst = mine("gate", 2)
                    for b in range(PB):
                        mm = pe.transpose(dst[0:QUAD, b * P:(b + 1) * P], CB[:, b, :], IDF[:, :])
                    mm.then_inc(gt_psum, 1)

                def expert_bias(l, new, part):
                    pe.wait_ge(gt_done, new)
                    dst = mine("bias", 2)
                    for b in range(PB):
                        mm = pe.matmul(dst[:, b * D:(b + 1) * D], CBT[0:E, b * P:(b + 1) * P], EB[:, :],
                                       start=True, stop=True)
                    mm.then_inc(eb_psum, 1)

                def experts(l, new, g):
                    b, o = g % PB, WE + (g // PB) * 2 * D
                    three_pass(mine(f"e{g}", 2)[:, :],
                               lambda c: XH[2][:, c, b * P:(b + 1) * P], lambda c: XL[2][:, c, b * P:(b + 1) * P],
                               lambda c: WH[2][:, c, o:o + 2 * D],
                               lambda c: WL[2][:, c, o:o + 2 * D]).then_inc(e_psum[g], 1)

                work = {"xt": xt, "ct": ct, "q": q, "k": k, "v": v, "max": row_max, "maxt": max_t,
                        "attend": attend, "z": z_tokens, "zt": z_transposed, "out": out_proj, "gate": gate_t,
                        "experts": experts, "bias": expert_bias}
                for kind, l, lag, part in UNITS:
                    if kind in work and active(i, lag):
                        work[kind](l, at[1 - lag], part)

            steps(pe, step)

        @block.scalar
        def _(act):
            for n, (l, c0, ncols, parts) in enumerate(pieces):
                act.wait_ge(stage_loaded[n % 3], staged[n])
                act.activation(WH[l][:, :, c0:c0 + ncols], stage(n, ncols), ACT.Copy).then_inc(w_hi_done, 1)
            act.wait_ge(setup_v, 3)

            def step(at, i, max_base, att_base):
                def rounded(dst, src, ready, new, done):
                    act.wait_ge(ready, new)
                    act.activation(dst[:, :, :].rearrange("p c t -> p (c t)"), src[:, :], ACT.Copy).then_inc(done, 1)

                def xt(l, new, part):
                    rounded(XH[l], bank("xt", l), xt_psum[l], new, xh_done[l])

                def ct(l, new, part):
                    rounded(CH, bank("ct", 1), ct_psum, new, ch_done)

                def q(l, new, part):
                    m, val = before(PROJ_ORDER, l, at, i)
                    if m is not None:
                        act.wait_ge(qb_done[m], val)
                        act.wait_ge(qh_done[m], val)
                    act.wait_ge(q_psum[l], new)
                    for t in range(C):
                        ins = act.activation(QF[:, t, :], bank("q", l)[:, t * TOK:(t + 1) * TOK], ACT.Identity,
                                             bias=QBI[:, l, t:t + 1], scale=SCALE)
                    ins.then_inc(qf_done[l], 1)
                    act.wait_ge(qf_done[l], new)
                    act.activation(QH[HALF[l]][:, :, :], QF[:, :, :], ACT.Copy).then_inc(qh_done[l], 1)

                def k(l, new, part):
                    m, val = before(PROJ_ORDER, l, at, i)
                    if m is not None:
                        act.wait_ge(kb_done[m], val)
                    act.wait_ge(k_psum[l], new)
                    for t in range(C):
                        ins = act.activation(KF[:, t, :], bank("k", l)[:, t * TOK:(t + 1) * TOK], ACT.Identity,
                                             bias=COLB[:, l, 1, t:t + 1])
                    ins.then_inc(kf_done[l], 1)
                    act.wait_ge(kf_done[l], new)
                    act.activation(KH[l][:, :, :], KF[:, :, :], ACT.Copy).then_inc(kh_done[l], 1)

                def v(l, new, part):
                    if l == 2:
                        act.wait_ge(gate_max, new)
                        for b in range(PB):
                            ins = act.activation(GE[:, b, :], GL[:, b, :], ACT.Exp, bias=GN[:, b:b + 1],
                                                 accum_out=GS[:, b:b + 1])
                        ins.then_inc(gate_exp, 1)

                def max_t(l, new, part):
                    act.wait_ge(mt_psum[l], new)
                    act.activation(MT[l][:, :], bank("maxt", l)[:, 0:P].bitcast(BF16), ACT.Copy).then_inc(mt_done[l], 1)

                def z_half(l, f):
                    act.wait_ge(pv_psum, att_base + (turn(ATT_ORDER, l, 4 * f + 3, i) + 1))
                    act.activation(ZA[f][:, :, :].rearrange("p k q -> p (k q)"), bank(f"pv{f}", l)[:, :],
                                   ACT.Copy).then_inc(za_done[(l, f)], 1)

                def attend(l, new, p):
                    if p in (5, 8):
                        z_half(l, p // 8)
                    if p == PAIRS:
                        return
                    g = turn(ATT_ORDER, l, p, i)
                    act.wait_ge(score_psum, att_base + (g + 1))
                    if i != 0 or g >= 3:
                        act.wait_ge(pv_psum, att_base + (g - 2))
                    act.activation(PR[slot(ATT_ORDER, l, p, i, 3)][:, :, :, :], SS[g % 2][:, :, :, :],
                                   ACT.Exp).then_inc(probs_done, 1)

                def z_transposed(l, new, part):
                    rounded(XH[l], bank("zt", l), zt_psum[l], new, zh_done[l])

                work = {"xt": xt, "ct": ct, "q": q, "k": k, "v": v, "maxt": max_t, "attend": attend,
                        "zt": z_transposed}
                for kind, l, lag, part in UNITS:
                    if kind in work and active(i, lag):
                        work[kind](l, at[1 - lag], part)

            steps(act, step)

        @block.vector
        def _(dve):
            own = [0]

            def setup_link(ins):
                own[0] += 1
                ins.then_inc(dve_setup, 1)
                dve.wait_ge(dve_setup, own[0])

            dve.wait_ge(const_loaded, CONSTS_LOADED)
            dve.tensor_copy(IDF[:, :], CONST[:, 0:P])
            dve.tensor_copy(IDB[:, :], CONST[:, 0:P])
            dve.tensor_scalar(MQ[0][:, :], CONST[:, P:2 * P], -MASKED, MASKED, ALU.mult, ALU.add)
            setup_link(dve.tensor_copy(MF[:, :], MI[:, :]))
            setup_link(dve.tensor_scalar(MQ[1][:, :], MF[:, :], 0.0, MASKED, ALU.is_equal, ALU.mult))
            dve.tensor_copy(SEL[:, :, :], CONST[:, 2 * P:2 * P + H].unsqueeze(2).to_broadcast([P, H, P]))
            setup_link(dve.tensor_scalar(QBI[:, :, :], COLB[:, :, 0, :], SCALE, None, ALU.mult))
            dve.memset(NHALF[:, :], -0.5)
            dve.memset(EPSC[:, :], EPS)
            setup_link(dve.memset(CB[:, :, :], 0.0))
            dve.memset(GN[:, :], 0.0).then_inc(setup_v, 1)
            for j in range(2):
                dve.wait_ge(setup_pe, j + 1)
                dve.tensor_copy(MK[j][:, :], WB[j][:, 0:P // 2].bitcast(BF16)).then_inc(setup_v, 1)
            for n, (l, c0, ncols, parts) in enumerate(pieces):
                dve.wait_ge(w_hi_done, n + 1)
                dve.tensor_tensor(WL[l][:, :, c0:c0 + ncols], stage(n, ncols),
                                  WH[l][:, :, c0:c0 + ncols].bitcast(F32), ALU.subtract).then_inc(w_lo_done, 1)
            dve.wait_ge(setup_p, 1)
            PAR = CONST[:, 2 * P + H:2 * P + H + 2]
            IOTA = CONST[:, 2 * P + H + 2:2 * P + H + 2 + E]

            def step(at, i, max_base, att_base):
                def carry(s, value):
                    dve.wait_ge(s, value)
                    dve.memset(SPARE[:, :], 0.0)

                per = sum(links(kind, l, part) for kind, l, _, part in UNITS)
                linked = [link_base(i) if i is not None else dve.snap(at[0] * per - (per * (DEPTH + 1) - link_base(DEPTH + 1))), 0]

                def link(ins, carried=False):
                    linked[1] += 1
                    ins.then_inc(vector_link, 1)
                    if carried:
                        carry(vector_link, linked[0] + linked[1])
                    else:
                        dve.wait_ge(vector_link, linked[0] + linked[1])

                def flat(t):
                    return t[:, :, :].rearrange("p c t -> p (c t)")

                def low(dst, src, hi, ready, new, done):
                    dve.wait_ge(ready, new)
                    dve.tensor_tensor(flat(dst), src[:, :], flat(hi).bitcast(F32), ALU.subtract).then_inc(done, 1)

                def xt(l, new, part):
                    low(XL[l], bank("xt", l), XH[l], xh_done[l], new, xl_done[l])

                def ct(l, new, part):
                    low(CL, bank("ct", 1), CH, ch_done, new, cl_done)

                def q(l, new, part):
                    dve.wait_ge(qf_done[l], new)
                    for h2 in range(2):
                        ins = dve.tensor_scalar(QBH[l][:, :, h2, :], QF[:, :, :], PAR[:, h2:h2 + 1], None, ALU.mult)
                    ins.then_inc(qbh_done[l], 1)

                def k(l, new, part):
                    kb, qb = KBH[HALF[l]], QBH[l]
                    dve.wait_ge(qbh_done[l], new)
                    for h2 in range(2):
                        ins = dve.scalar_tensor_tensor(out=QBL[l][:, :, h2, :], in0=QF[:, :, :],
                                                       scalar=PAR[:, h2:h2 + 1], in1=qb[:, :, h2, :].bitcast(F32),
                                                       op0=ALU.mult, op1=ALU.subtract)
                    ins.then_inc(qb_done[l], 1)
                    dve.wait_ge(kf_done[l], new)
                    for h2 in range(2):
                        dve.tensor_scalar(kb[:, :, h2, :], KF[:, :, :], PAR[:, h2:h2 + 1], None, ALU.mult)
                    dve.wait_ge(kh_done[l], new)
                    dve.tensor_tensor(KL[l][:, :, :], KF[:, :, :], KH[l][:, :, :].bitcast(F32),
                                      ALU.subtract).then_inc(kb_done[l], 1)

                def v(l, new, part):
                    for b in range(PB):
                        if l == 2:
                            dve.wait_ge(v_psum[(l, b)], new)
                            src = bank(("v", "v1")[b], l)
                            dve.tensor_tensor(GL[:, b, :], src[:, D:VG], RB[:, RB_V[2] + D:RB_V[2] + VG], ALU.add)
                            o = 0
                        else:
                            if b == 0:
                                dve.wait_ge(v_psum[(l, 0)], new)
                            src = bank("v", l)
                            o = b * D
                        ins = dve.tensor_tensor(VA[l][:, b, :, 0:DH],
                                                src[:, o:o + D].rearrange("p (h d) -> p h d", h=H),
                                                RB[:, RB_V[l]:RB_V[l] + D].rearrange("p (h d) -> p h d", h=H), ALU.add)
                        if l == 2:
                            ins.then_inc(v_done[(l, b)], 1)
                    if l < 2:
                        ins.then_inc(v_done[(l, 0)], 1)
                    else:
                        dve.wait_ge(v_done[(2, 1)], new)
                        dve.tensor_reduce(GN[:, :], GL[:, :, :], AX.X, ALU.max, negate=True).then_inc(gate_max, 1)

                def gate_top(n):
                    dve.wait_ge(gate_exp, n)
                    link(dve.reciprocal(GR[:, :], GS[:, :]))
                    for b in range(PB):
                        ins = dve.tensor_scalar(GP[:, b, :], GE[:, b, :], GR[:, b:b + 1], None, ALU.mult)
                    link(ins, carried=True)
                    for b in range(PB):
                        ins = dve.max(GT[:, b, :], GP[:, b, :])
                    link(ins, carried=True)
                    for b in range(PB):
                        ins = dve.max_index(GI[:, b, :], GT[:, b, :], GP[:, b, :])
                    link(ins)
                    link(dve.tensor_copy(GF[:, :, :], GI[:, :, :]))
                    for b in range(PB):
                        dve.tensor_scalar(G1[:, b, :], IOTA, GF[:, b, 0:1], GT[:, b, 0:1], ALU.is_equal, ALU.mult)
                        ins = dve.tensor_scalar(G2[:, b, :], IOTA, GF[:, b, 1:2], GT[:, b, 1:2], ALU.is_equal,
                                                ALU.mult)
                    link(ins)
                    dve.tensor_tensor(CB[:, :, 0:E], G1[:, :, :], G2[:, :, :], ALU.add).then_inc(combine_done, 1)

                def row_max(l, new, p):
                    g = turn(MAX_ORDER, l, p, i)
                    dve.wait_ge(max_psum, max_base + (g + 1))
                    dve.tensor_reduce(NM[:, :, 2 * p:2 * p + 2], SM[g % 2][:, :, :, :], AX.X, ALU.max,
                                      negate=True).then_inc(max_read, 1)
                    if l == 2 and p == 1:
                        gate_top(new)
                    if p < PAIRS - 1:
                        return
                    m, val = before(MAX_ORDER, l, at, i)
                    if m is not None:
                        dve.wait_ge(mt_psum[m], val)
                    dve.wait_ge(max_read, max_base + (g + 1))
                    for b in range(PB):
                        ins = dve.tensor_copy(NMB[:, b, :, 0, :], NM[:, b, :].unsqueeze(1).to_broadcast([P, 4, H]))
                    link(ins)
                    for b in range(PB):
                        ins = dve.tensor_tensor(NMB[:, b, :, 1, :], NM[:, b, :].unsqueeze(1).to_broadcast([P, 4, H]),
                                                NMB[:, b, :, 0, :], ALU.subtract)
                    ins.then_inc(nm_done[l], 1)

                def z_tokens(l, new, f):
                    dve.wait_ge(z_psum[(l, f)], new)
                    src = bank(f"z{f}", l)[:, :].rearrange("q (p b h d) -> q p b h d", p=4, b=PB, h=2)
                    rz = RZ[:, :, 4 * f:4 * f + 4, :]
                    for b in range(PB):
                        ins = dve.reciprocal(rz[:, b, :, :].unsqueeze(3), src[:, :, b, :, DH:DH + 1])
                    link(ins)
                    for b in range(PB):
                        ins = dve.tensor_tensor(Z[l][:, b, 8 * f:8 * f + 8, :].rearrange("q (p h) d -> q p h d", p=4),
                                                src[:, :, b, :, 0:DH],
                                                rz[:, b, :, :].unsqueeze(3).to_broadcast([P, 4, 2, DH]), ALU.mult)
                    ins.then_inc(z_done[(l, f)], 1)

                def z_transposed(l, new, part):
                    low(XL[l], bank("zt", l), XH[l], zh_done[l], new, zl_done[l])

                def normalise(l, lag):
                    new, old = at[1 - lag], at[-lag]
                    for b in range(PB):
                        ins = dve.bn_stats(ST[:, l, b, :], XB[l][:, b, :])
                    link(ins, carried=True)
                    for b in range(PB):
                        ins = dve.bn_aggr(MV[:, l, b, :], ST[:, l, b, :])
                    ins.then_inc(mv_done[l], 1)
                    dst = X[l + 1] if l < 2 else XB[2]
                    if l < 2 and (i is None or i > lag):
                        dve.wait_ge(xb_done[1] if l == 0 else eb_done, old)
                        dve.wait_ge(xt_psum[l + 1], old)
                    dve.wait_ge(rs_done[l], new)
                    for b in range(PB):
                        ins = dve.tensor_scalar(dst[:, b, :], XB[l][:, b, :], MV[:, l, b, 0:1], RS[:, l, b:b + 1],
                                                ALU.subtract, ALU.mult)
                    ins.then_inc(norm_done[l], 1)

                def out_proj(l, new, lag):
                    dve.wait_ge(o_psum[l], new)
                    dve.wait_ge(xb_done[l], new)
                    xb = XB[l][:, :, :].rearrange("p b d -> p (b d)")
                    dve.tensor_tensor(xb, bank("out", l)[:, :], xb, ALU.add).then_inc(sum_done[l], 1)
                    dve.wait_ge(sum_done[l], new)
                    normalise(l, lag)

                def gate_t(l, new, part):
                    dve.wait_ge(gt_psum, new)
                    dve.tensor_copy(CBT[:, :], bank("gate", 2)[0:QUAD, 0:TOK]).then_inc(gt_done, 1)

                def expert_bias(l, new, lag):
                    if i is None or i > lag:
                        dve.wait_ge(out_stored, at[-lag] * 16)
                    dve.wait_ge(eb_psum, new)
                    dve.tensor_tensor(XB[2][:, :, :].rearrange("p b d -> p (b d)"), bank("bias", 2)[:, :],
                                      X[2][:, :, :].rearrange("p b d -> p (b d)"), ALU.add).then_inc(eb_done, 1)

                def experts(l, new, g):
                    b, acc = g % PB, XB[2]
                    dve.wait_ge(e_psum[g], new)
                    for half in range(2):
                        e = 2 * (g // PB) + half
                        if half:
                            dve.wait_ge(e_half[g], new)
                        elif g < PB:
                            dve.wait_ge(eb_done, new)
                        else:
                            dve.wait_ge(e_done[g - PB], new)
                        dve.scalar_tensor_tensor(
                            out=acc[:, b, :], in0=bank(f"e{g}", 2)[:, half * D:(half + 1) * D],
                            scalar=CB[:, b, e:e + 1], in1=acc[:, b, :], op0=ALU.mult,
                            op1=ALU.add).then_inc((e_done if half else e_half)[g], 1)

                def finish(l, new, lag):
                    for g in range(E - PB, E):
                        dve.wait_ge(e_done[g], new)
                    dve.tensor_tensor(XB[2][:, :, :], XB[2][:, :, :],
                                      Z[2][:, :, :, :].rearrange("p b h d -> p b (h d)"),
                                      ALU.add).then_inc(sum_done[2], 1)
                    dve.wait_ge(sum_done[2], new)
                    normalise(2, lag)

                work = {"xt": xt, "ct": ct, "q": q, "k": k, "v": v, "max": row_max, "z": z_tokens,
                        "zt": z_transposed, "out": out_proj, "gate": gate_t, "experts": experts, "finish": finish,
                        "bias": expert_bias}
                for kind, l, lag, part in UNITS:
                    if kind in work and active(i, lag):
                        work[kind](l, at[1 - lag], lag if kind in ("out", "finish", "bias") else part)

            steps(dve, step)

        @block.gpsimd
        def _(pool):
            pool.wait_ge(w_lo_done, len(pieces))
            for l in range(NL):
                ins = pool.memset(VA[l][:, :, :, DH:QUAD], 1.0)
            ins.then_inc(setup_p, 1)
            pool.wait_ge(setup_v, 1)

            def step(at, i, max_base, att_base):
                def residual(l, lag):
                    new = at[1 - lag]
                    if l == 0:
                        pool.wait_ge(x_loaded, new * 16)
                    else:
                        pool.wait_ge(norm_done[l - 1], new)
                    if i is None or i > lag:
                        pool.wait_ge(norm_done[l], at[-lag])
                    for b in range(PB):
                        ins = pool.tensor_tensor(XB[l][:, b, :], X[l][:, b, :], RB[:, RB_O[l]:RB_O[l] + D], ALU.add)
                    ins.then_inc(xb_done[l], 1)

                def rstd(l, lag):
                    new = at[1 - lag]
                    pool.wait_ge(mv_done[l], new)
                    pool.tensor_tensor(VE[:, l, :], MV[:, l, :, 1], EPSC[:, :], ALU.add).then_inc(ve_done[l], 1)
                    pool.wait_ge(ve_done[l], new)
                    pool.tensor_tensor(RS[:, l, :], VE[:, l, :], NHALF[:, :], ALU.pow).then_inc(rs_done[l], 1)

                for kind, l, lag, part in UNITS:
                    if active(i, lag):
                        if kind == "xt" and l < 2:
                            residual(l, lag)
                        if kind in ("out", "finish"):
                            rstd(l, lag)

            steps(pool, step)


def kernel(x, ctx_1024, mask_1x1xSxS2_ik0, L0_attn_W_qkv, L0_attn_b_qkv, L0_attn_W_proj, L0_attn_b_proj,
           L0_xattn_wq, L0_xattn_bq, L0_xattn_wk, L0_xattn_bk, L0_xattn_wv, L0_xattn_bv, L0_xattn_wo, L0_xattn_bo,
           L0_ffn_W_qkv, L0_ffn_b_qkv, L0_ffn_W_gate, L0_ffn_b_gate, L0_ffn_W_experts, L0_ffn_b_experts):
    import numpy as np
    import concourse.bacc as bacc
    from concourse.bass_utils import run_bass_kernel_spmd

    def a(v):
        return np.asarray(v)

    part = np.arange(P)
    consts = np.concatenate([
        np.eye(P), np.tril(np.ones((P, P))), part[:, None] % H == np.arange(H)[None, :],
        part[:, None] % QUAD // DH == np.arange(2)[None, :], np.tile(np.arange(E), (P, 1)),
    ], axis=1).astype(np.float32)
    row = np.concatenate([a(L0_attn_b_qkv)[2 * D:], a(L0_attn_b_proj), a(L0_xattn_bv), a(L0_xattn_bo),
                          a(L0_ffn_b_qkv)[2 * D:], a(L0_ffn_b_gate)])
    rows = np.ascontiguousarray(np.broadcast_to(row[None, :], (P, RB_COLS)))
    col = np.stack([a(L0_attn_b_qkv)[:2 * D], np.concatenate([a(L0_xattn_bq), a(L0_xattn_bk)]),
                    a(L0_ffn_b_qkv)[:2 * D]])
    cols = np.ascontiguousarray(col.reshape(NL * 2 * C, P).T)
    arrays = {
        "x": a(x), "ctx": a(ctx_1024), "mask": np.ascontiguousarray(a(mask_1x1xSxS2_ik0).reshape(P, P)),
        "qkv0": a(L0_attn_W_qkv), "o0": a(L0_attn_W_proj),
        "q1": np.ascontiguousarray(a(L0_xattn_wq).T), "k1": np.ascontiguousarray(a(L0_xattn_wk).T),
        "v1": np.ascontiguousarray(a(L0_xattn_wv).T), "o1": np.ascontiguousarray(a(L0_xattn_wo).T),
        "qkv2": a(L0_ffn_W_qkv), "gate": a(L0_ffn_W_gate), "experts": a(L0_ffn_W_experts),
        "eb": a(L0_ffn_b_experts), "rows": rows, "cols": cols, "consts": consts,
    }
    nc = bacc.Bacc("TRN2", target_bir_lowering=False, num_devices=1)
    t = {n: nc.dram_tensor(f"in_{n}", v.shape, mybir.dt.from_np(v.dtype), kind="ExternalInput").ap()
         for n, v in arrays.items()}
    out = nc.dram_tensor("out_0", (B, P, D), F32, kind="ExternalOutput").ap()
    decoder(nc, t["x"], t["ctx"], t["mask"], t, t["rows"], t["cols"], t["eb"], t["consts"], out)
    r = run_bass_kernel_spmd(nc, [{f"in_{n}": v for n, v in arrays.items()}], core_ids=[0])
    return r.results[0]["out_0"]
```

```python
from contextlib import ExitStack

import concourse.bass as bass
from concourse import mybir
from concourse.alu_op_type import AluOpType as ALU

ACT = mybir.ActivationFunctionType
F32 = mybir.dt.float32
F32R = mybir.dt.float32r
BF16 = mybir.dt.bfloat16
U32 = mybir.dt.uint32
AX = mybir.AxisListType

P = 128
D = 256
H = 16
DH = D // H
E = 8
B = 32
PB = 2
TOK = PB * P
NSTEP = B // PB
NL = 3
C = D // P
QUAD = 32
SCALE = DH ** -0.5
EPS = 1e-5
MASKED = -(2.0 ** 100)
PARTS = 3
HC = P // DH
STACK_FROM = {"q": [(0, 3), (0, 2), (0, 1)], "k": [(0, 3), (1, 3), (2, 3)]}
PLACE = {"q": [0, 1, 2], "k": [2, 1, 0]}
ROWS = DH * sum(b - a for a, b in STACK_FROM["q"])
VG = D + E

WQ, WK, WV, WO = 0, D, 2 * D, 3 * D
WE = 2 * D + VG
WCOLS = [4 * D, 4 * D, WE + E * D]
RB_V = [0, 2 * D, 4 * D]
RB_O = [D, 3 * D]
RB_COLS = 4 * D + VG

PAIRS = H // 2
STEP_TICKS = 24
LAYER_TIMES = [
    [('xt', 0, 4.302), ('q', 0, 5.35), ('k', 0, 7.352), ('v', 0, 8.767), ('max', 0, 11.612), ('max', 1, 12.136), ('max', 2, 12.66), ('max', 3, 13.184), ('max', 4, 13.708), ('max', 5, 14.232), ('max', 6, 14.756), ('max', 7, 15.28), ('maxt', 0, 15.915), ('stack', 0, 8.777), ('maxload', 0, 15.925), ('attend', 0, 16.05), ('attend', 1, 17.02), ('attend', 2, 17.99), ('attend', 3, 18.96), ('attend', 4, 19.93), ('attend', 5, 20.9), ('attend', 6, 21.87), ('attend', 7, 22.84), ('attend', 8, 23.81), ('z', 0, 22.627), ('z', 1, 24.902), ('zt', 0, 25.814), ('out', 0, 26.056)],
    [('xt', 0, 34.879), ('q', 0, 37.35), ('k', 0, 37.505), ('v', 0, 38.843), ('max', 0, 42.496), ('max', 1, 43.02), ('max', 2, 43.544), ('max', 3, 44.068), ('max', 4, 44.592), ('max', 5, 45.116), ('max', 6, 45.64), ('max', 7, 46.164), ('maxt', 0, 47.663), ('stack', 0, 38.853), ('maxload', 0, 47.673), ('attend', 0, 48.05), ('attend', 1, 49.02), ('attend', 2, 49.99), ('attend', 3, 50.96), ('attend', 4, 51.93), ('attend', 5, 52.9), ('attend', 6, 53.87), ('attend', 7, 54.84), ('attend', 8, 55.81), ('z', 0, 54.488), ('z', 1, 56.52), ('zt', 0, 57.074), ('out', 0, 58.58), ('ct', 0, 36.58)],
    [('xt', 0, 68.481), ('q', 0, 69.35), ('k', 0, 69.95), ('v', 0, 70.914), ('max', 0, 75.25), ('max', 1, 75.774), ('max', 2, 76.298), ('max', 3, 76.822), ('max', 4, 77.346), ('max', 5, 77.87), ('max', 6, 78.394), ('max', 7, 78.918), ('maxt', 0, 80.005), ('stack', 0, 70.924), ('maxload', 0, 80.015), ('attend', 0, 80.05), ('attend', 1, 81.02), ('attend', 2, 81.99), ('attend', 3, 82.96), ('attend', 4, 83.93), ('attend', 5, 84.9), ('attend', 6, 85.87), ('attend', 7, 86.84), ('attend', 8, 87.81), ('z', 0, 86.475), ('z', 1, 89.74), ('gate', 0, 76.95), ('bias', 0, 77.45), ('experts', 0, 77.698), ('experts', 1, 79.698), ('experts', 2, 81.498), ('experts', 3, 83.437), ('experts', 4, 85.55), ('experts', 5, 87.35), ('experts', 6, 89.35), ('experts', 7, 91.15), ('finish', 0, 92.65), ('store', 0, 93.65)],
]
TIMETABLE = sorted((t % STEP_TICKS, l, kind, int(t // STEP_TICKS), part)
                   for l in range(NL) for kind, part, t in LAYER_TIMES[l])
UNITS = [(kind, l, lag, part) for _, l, kind, lag, part in TIMETABLE]
DEPTH = max(u[2] for u in UNITS)
PROJ_ORDER = [u[1:3] for u in UNITS if u[0] == "q"]
MAX_ORDER = [u[1:3] for u in UNITS if u[0] == "max" and u[3] == 0]
ATT_ORDER = [u[1:3] for u in UNITS if u[0] == "attend" and u[3] == 0]
WORK_BANKS = 4


def work_uses():
    uses = []
    for kind, l, lag, part in UNITS:
        if kind in ("xt", "ct", "q", "k", "v", "maxt", "gate", "bias", "zt", "out"):
            uses.append((kind, l, lag))
        if kind == "v" and l == 2:
            uses.append(("v1", l, lag))
        if kind == "attend" and part in (1, 5):
            uses.append((f"pv{part // 4}", l, lag))
        if kind == "z":
            uses.append((f"z{part}", l, lag))
        if kind == "experts":
            uses.append((f"e{part}", 2, lag))
    return uses


USES = work_uses()
BANK_OF = {}
for _use in USES:
    BANK_OF[_use[:2]] = 0 if _use[0].startswith("pv") else 1 + sum(v > 0 for v in BANK_OF.values()) % (WORK_BANKS - 1)
assert len(BANK_OF) == len(USES)


def active(i, lag):
    return i is None or 0 <= i - lag < NSTEP


def decoder(nc, x, ctx, mask, w, rows, cols, eb, consts, split, out):
    with ExitStack() as stack:
        def sb(name, shape, dt=F32):
            return stack.enter_context(nc.sbuf_tensor(name, shape, dt))

        def sem(name):
            return stack.enter_context(nc.semaphore(name))

        def per_layer(name, layers=range(NL)):
            return {l: sem(f"{name}_{l}") for l in layers}

        def bufs(name, shape, dt=F32, n=NL):
            return [sb(f"{name}{l}", shape, dt) for l in range(n)]

        X = bufs("x", [P, PB, D])
        XB = bufs("res", [P, PB, D])
        CTX = sb("ctx", [P, PB, D])
        XH = bufs("x_hi", [P, C, TOK], F32R)
        XL = bufs("x_lo", [P, C, TOK], F32R)
        CH = sb("c_hi", [P, C, TOK], F32R)
        CL = sb("c_lo", [P, C, TOK], F32R)
        QF = sb("q_full", [P, C, TOK])
        KF = sb("k_full", [P, C, TOK])
        QP = sb("q_parts", [P, PARTS, C, TOK], BF16)
        KP = sb("k_parts", [P, PARTS, C, TOK], BF16)
        QS = bufs("q_stack", [ROWS, HC, C, TOK], BF16)
        KS = bufs("k_stack", [ROWS, HC, C, TOK], BF16)
        VA = bufs("v_ones", [P, PB, H, QUAD])
        NM = sb("neg_max", [P, PB, H])
        NMB = sb("neg_max_parts", [P, PB, 4, 2, H], BF16)
        MT = bufs("neg_max_t", [P, TOK], BF16)
        PR = bufs("probs", [P, PB, 2, P], F32, 3)
        ZA = bufs("z_aug", [P, 4, P], F32, 2)
        Z = bufs("z", [P, PB, H, DH])
        RZ = sb("z_recip", [P, PB, PAIRS, 2])
        ST = sb("bn_stats", [P, NL, PB, 6])
        MV = sb("mean_var", [P, NL, PB, 2])
        VE = sb("var_eps", [P, NL, PB])
        RS = sb("rstd", [P, NL, PB])
        GL = sb("gate_logits", [P, PB, E])
        GN = sb("gate_neg_max", [P, PB])
        GE = sb("gate_exp", [P, PB, E])
        GS = sb("gate_sum", [P, PB])
        GR = sb("gate_recip", [P, PB])
        GP = sb("gate_probs", [P, PB, E])
        GT = sb("gate_top", [P, PB, 8])
        GI = sb("gate_index", [P, PB, 8], U32)
        GF = sb("gate_index_f", [P, PB, 8])
        G1 = sb("combine_first", [P, PB, E])
        G2 = sb("combine_second", [P, PB, E])
        CB = sb("combine", [P, PB, QUAD])
        CBT = sb("combine_t", [QUAD, TOK])
        WH = [sb(f"w_hi{l}", [P, C, WCOLS[l]], F32R) for l in range(NL)]
        WL = [sb(f"w_lo{l}", [P, C, WCOLS[l]], F32R) for l in range(NL)]
        IDF = sb("ident_f", [P, P])
        IDB = sb("ident_b", [P, P], BF16)
        CONST = sb("consts", [P, P + P + H + E])
        MI = sb("mask_int", [P, P], mybir.dt.int32)
        MF = sb("mask_f", [P, P])
        MQ = bufs("mask_qk", [P, P], BF16, 2)
        MK = bufs("mask_kq", [P, P], BF16, 2)
        SEL = sb("head_rows", [P, H], BF16)
        RB = sb("row_bias", [P, RB_COLS])
        COLB = sb("col_bias", [P, NL, 2, C])
        QBI = sb("q_bias_scaled", [P, NL, C])
        EB = sb("expert_bias", [E, D])
        NHALF = sb("minus_half", [P, PB])
        EPSC = sb("epsilon", [P, PB])
        SPARE = sb("spare", [P, 1])

        SM = [stack.enter_context(nc.psum_tensor(f"max_scores{i}", [P, PB, 2, P], F32)) for i in range(2)]
        SS = [stack.enter_context(nc.psum_tensor(f"scores{i}", [P, PB, 2, P], F32)) for i in range(2)]
        WB = [stack.enter_context(nc.psum_tensor(f"work{i}", [P, 512], F32)) for i in range(WORK_BANKS)]

        def bank(name, l):
            return WB[BANK_OF[(name, l)]]

        const_loaded = sem("const_loaded")
        stage_loaded = [sem(f"stage_loaded{n}") for n in range(3)]
        w_hi_done = sem("w_hi_done")
        w_lo_done = sem("w_lo_done")
        setup_v = sem("setup_v")
        setup_pe = sem("setup_pe")
        setup_p = sem("setup_p")
        dve_setup = sem("dve_setup")
        x_loaded = sem("x_loaded")
        ctx_loaded = sem("ctx_loaded")
        out_stored = sem("out_stored")
        xt_psum = per_layer("xt_psum")
        xh_done = per_layer("xh_done")
        xl_done = per_layer("xl_done")
        xb_done = per_layer("xb_done", (0, 1))
        ct_psum, ch_done, cl_done = sem("ct_psum"), sem("ch_done"), sem("cl_done")
        q_psum = per_layer("q_psum")
        k_psum = per_layer("k_psum")
        v_psum = {(l, b): sem(f"v_psum_{l}{b}") for l, b in ((0, 0), (1, 0), (2, 0), (2, 1))}
        v_done = {(l, b): sem(f"v_done_{l}{b}") for l, b in ((0, 0), (1, 0), (2, 0), (2, 1))}
        qf_done = per_layer("qf_done")
        kf_done = per_layer("kf_done")
        nm_done = per_layer("nm_done")
        mt_psum = per_layer("mt_psum")
        mt_done = per_layer("mt_done")
        za_done = {(l, f): sem(f"za_done_{l}{f}") for l in range(NL) for f in range(2)}
        z_psum = {(l, f): sem(f"z_psum_{l}{f}") for l in range(NL) for f in range(2)}
        z_done = {(l, f): sem(f"z_done_{l}{f}") for l in range(NL) for f in range(2)}
        zt_psum = per_layer("zt_psum", (0, 1))
        zh_done = per_layer("zh_done", (0, 1))
        zl_done = per_layer("zl_done", (0, 1))
        o_psum = per_layer("o_psum", (0, 1))
        sum_done = per_layer("sum_done")
        mv_done = per_layer("mv_done")
        ve_done = per_layer("ve_done")
        rs_done = per_layer("rs_done")
        norm_done = per_layer("norm_done")
        max_psum = sem("max_psum")
        max_read = sem("max_read")
        score_psum = sem("score_psum")
        probs_done = sem("probs_done")
        pv_psum = sem("pv_psum")
        hi_done, rest_done, mid_done, low_done, stored = (
            {x: sem(f"{x}_{name}") for x in "qk"} for name in ("hi", "rest", "mid", "low", "stored"))
        stacked = {(x, l): sem(f"{x}_stacked_{l}") for x in "qk" for l in range(NL)}
        vector_link = sem("vector_link")
        gate_max, gate_exp, combine_done = sem("gate_max"), sem("gate_exp"), sem("combine_done")
        gt_psum, gt_done, eb_psum, eb_done = sem("gt_psum"), sem("gt_done"), sem("eb_psum"), sem("eb_done")
        e_psum = [sem(f"e_psum_{g}") for g in range(E)]
        e_half = [sem(f"e_half_{g}") for g in range(E)]

        e_done = [sem(f"e_done_{g}") for g in range(E)]

        read_by = {}
        for l in range(NL):
            read_by[("xt", l)] = xl_done[l]
            read_by[("q", l)] = qf_done[l]
            read_by[("k", l)] = kf_done[l]
            read_by[("v", l)] = v_done[(l, 0)]
            read_by[("maxt", l)] = mt_done[l]
            for f in range(2):
                read_by[(f"pv{f}", l)] = za_done[(l, f)]
                read_by[(f"z{f}", l)] = z_done[(l, f)]
        for l in (0, 1):
            read_by[("zt", l)] = zl_done[l]
            read_by[("out", l)] = sum_done[l]
        read_by[("ct", 1)] = cl_done
        read_by[("v1", 2)] = v_done[(2, 1)]
        read_by[("gate", 2)] = gt_done
        read_by[("bias", 2)] = eb_done
        for g in range(E):
            read_by[(f"e{g}", 2)] = e_done[g]

        def steps(eng, body, end=NSTEP):
            def straight(i):
                body({c: i + c for c in range(-DEPTH, 2)}, i, ring_base(MAX_ORDER, i), ring_base(ATT_ORDER, i),
                     ring_base(PROJ_ORDER, i) // PAIRS)
            full = DEPTH + 1
            for i in range(full):
                straight(i)
            with eng.Fori(full, end) as i:
                at = {c: eng.snap(i + c) for c in range(-DEPTH, 2)}
                per = NL * PAIRS
                body(at, None, eng.snap(i * per - (per * full - ring_base(MAX_ORDER, full))),
                     eng.snap(i * per - (per * full - ring_base(ATT_ORDER, full))),
                     eng.snap(i * NL - (NL * full - ring_base(PROJ_ORDER, full) // PAIRS)))
            for i in range(end, NSTEP + DEPTH):
                straight(i)

        def ring_base(order, i):
            return PAIRS * sum(active(j, lag) for j in range(i) for _, lag in order)

        def links(kind, l, part):
            return {"z": 1, "out": 1, "finish": 1}.get(kind, 0) + (kind == "max") * ((part == PAIRS - 1) + 6 * (l == 2 and part == 1))

        def link_base(i):
            return sum(links(kind, l, part) for j in range(i) for kind, l, lag, part in UNITS if active(j, lag))

        def turn(order, l, p, i):
            return PAIRS * [m for m, lag in order if active(i, lag)].index(l) + p

        def proj_turn(l, i):
            return turn(PROJ_ORDER, l, 0, i) // PAIRS + 1

        def slot(order, l, p, i, n):
            return (ring_base(order, DEPTH + 1 if i is None else i) + turn(order, l, p, i)) % n

        def before(order, l, at, i):
            n = [m for m, _ in order].index(l)
            for m, lag in reversed(order[:n]):
                if active(i, lag):
                    return m, at[1 - lag]
            for m, lag in reversed(order):
                if active(i if i is None else i - 1, lag):
                    return m, at[-lag]
            return None, None

        def claim(eng, name, l, at, i):
            mine, uses = BANK_OF[(name, l)], [u[:2] for u in USES]
            here = uses.index((name, l))
            for use in reversed(USES[:here]):
                if BANK_OF[use[:2]] == mine and active(i, use[2]):
                    return eng.wait_ge(read_by[use[:2]], at[1 - use[2]])
            for use in reversed(USES):
                if BANK_OF[use[:2]] == mine and active(i if i is None else i - 1, use[2]):
                    return eng.wait_ge(read_by[use[:2]], at[-use[2]])

        x_v = x.rearrange("(n b) s d -> n s b d", b=PB)
        ctx_v = ctx.rearrange("(n b) s d -> n s b d", b=PB)
        out_v = out.rearrange("(n b) s d -> n s b d", b=PB)

        def cols_of(ap, a, b):
            return ap.rearrange("(c p) n -> p c n", p=P)[:, :, a:b]

        pieces = [
            (0, WQ, 2 * D, [(0, cols_of(w["qkv0"], 0, 2 * D))]),
            (0, WV, 2 * D, [(0, cols_of(w["qkv0"], 2 * D, 3 * D)), (D, cols_of(w["o0"], 0, D))]),
            (1, WQ, 2 * D, [(0, cols_of(w["q1"], 0, D)), (D, cols_of(w["k1"], 0, D))]),
            (1, WV, 2 * D, [(0, cols_of(w["v1"], 0, D)), (D, cols_of(w["o1"], 0, D))]),
            (2, WQ, 2 * D, [(0, cols_of(w["qkv2"], 0, 2 * D))]),
            (2, WV, VG, [(0, cols_of(w["qkv2"], 2 * D, 3 * D)), (D, cols_of(w["gate"], 0, E))]),
        ]
        for g in range(E // 2):
            pieces.append((2, WE + 2 * g * D, 2 * D,
                           [(j * D, cols_of(w["experts"][2 * g + j], 0, D)) for j in range(2)]))
        staged = [16 * sum(len(q[3]) for q in pieces[n % 3:n + 1:3]) for n in range(len(pieces))]

        def stage(n, ncols):
            return VA[n % 3][:, :, :, :].rearrange("p b h d -> p (b h d)")[:, 0:C * ncols].rearrange(
                "p (c n) -> p c n", c=C)

        block = stack.enter_context(nc.Block())

        @block.sync
        def _(sp):
            n_const = 0
            for dst, src in ((CONST[:, :], consts), (MI[:, :], mask), (RB[:, :], rows),
                             (COLB[:, :, :, :].rearrange("p l q c -> p (l q c)"), cols),
                             (EB[:, :], eb)):
                sp.dma_start(dst, src).then_inc(const_loaded, 16)
                n_const += 16
            sp.dma_start(X[0][:, :, :], x_v[0]).then_inc(x_loaded, 16)
            sp.dma_start(CTX[:, :, :], ctx_v[0]).then_inc(ctx_loaded, 16)
            for n, (l, c0, ncols, parts) in enumerate(pieces):
                if n >= 3:
                    sp.wait_ge(w_lo_done, n - 2)
                for off, src in parts:
                    sp.dma_start(stage(n, ncols)[:, :, off:off + src.shape[2]], src).then_inc(stage_loaded[n % 3], 16)

            def step(at, i, max_base, att_base, proj_base):
                def value(v):
                    if i is None:
                        sp.compute_val(v)
                    return v

                turns = {l: value(proj_base + proj_turn(l, i)) for l, lag in PROJ_ORDER if active(i, lag)}
                all_stored = {l: value((proj_base + proj_turn(l, i)) * (16 * PARTS)) for l in turns}
                all_stacked = {c: value(at[c] * (16 * PARTS)) for c in at}

                def store_part(x, l, k):
                    done = (hi_done, mid_done, low_done)[k]
                    m, val = before(PROJ_ORDER, l, {c: c for c in at}, i)
                    if k == 0 and m is not None:
                        sp.wait_ge(stacked[(x, m)], all_stacked[val])
                    sp.wait_ge(done[x], turns[l])
                    sp.dma_start(split[x][:, PLACE[x][k], :, :],
                                 (QP if x == "q" else KP)[:, k, :, :].rearrange("p c t -> p (c t)")
                                 ).then_inc(stored[x], 16)

                def load_stack(x, l, lag):
                    dst, row = (QS if x == "q" else KS)[l], 0
                    sp.wait_ge(stored[x], all_stored[l])
                    if i is None or i > lag:
                        sp.wait_ge(z_psum[(l, 1)], at[-lag])
                    for a, b in STACK_FROM[x]:
                        end = row + (b - a) * DH
                        sp.dma_start(dst[row:end, :, :, :].rearrange("r h c t -> r h (c t)"),
                                     split[x][:, a:b, :, :].rearrange("h s r t -> h (s r) t").rearrange("h q t -> q h t")).then_inc(stacked[(x, l)], 16)
                        row = end

                for kind, l, lag, part in UNITS:
                    if not active(i, lag):
                        continue
                    new = at[1 - lag]
                    if kind == "q":
                        store_part("q", l, 0)
                    if kind == "k":
                        store_part("k", l, 0)
                        store_part("q", l, 1)
                    if kind == "v":
                        store_part("q", l, 2)
                        store_part("k", l, 1)
                        store_part("k", l, 2)
                        load_stack("q", l, lag)
                        load_stack("k", l, lag)
                    if kind == "q" and l == 0 and (i is None or i < NSTEP - 1):
                        sp.wait_ge(xt_psum[0], new)
                        sp.wait_ge(xb_done[0], new)
                        sp.dma_start(X[0][:, :, :], x_v[new]).then_inc(x_loaded, 16)
                    if kind == "q" and l == 1 and (i is None or i - lag < NSTEP - 1):
                        sp.wait_ge(ct_psum, new)
                        sp.dma_start(CTX[:, :, :], ctx_v[new]).then_inc(ctx_loaded, 16)
                    if kind == "store":
                        sp.wait_ge(norm_done[2], new)
                        sp.dma_start(out_v[at[-lag]], XB[2][:, :, :]).then_inc(out_stored, 16)

            steps(sp, step, NSTEP - 1)
            sp.wait_ge(out_stored, 16 * NSTEP)
            sp.wait_ge(const_loaded, n_const)
            for x in "qk":
                sp.wait_ge(stored[x], 16 * PARTS * NL * NSTEP)

        CONSTS_LOADED = 16 * 5

        @block.tensor
        def _(pe):
            pe.wait_ge(setup_v, 1)
            for j in range(2):
                pe.transpose(WB[j][:, 0:P // 2].bitcast(BF16), MQ[j][:, :], IDB[:, :]).then_inc(setup_pe, 1)
            pe.wait_ge(setup_v, 3)
            pe.wait_ge(setup_p, 1)
            pe.wait_ge(w_lo_done, len(pieces))

            def three_pass(dst, lhs_h, lhs_l, rhs_h, rhs_l):
                for c in range(C):
                    mm = None
                    for k, (a, b) in enumerate(((lhs_h, rhs_h), (lhs_h, rhs_l), (lhs_l, rhs_h))):
                        mm = pe.matmul(dst, a(c), b(c), start=(c == 0 and k == 0), stop=(c == C - 1 and k == 2))
                return mm

            def transpose_tokens(src, dst):
                for b in range(PB):
                    for c in range(C):
                        mm = pe.transpose(dst[:, c * TOK + b * P:c * TOK + (b + 1) * P],
                                          src[:, b, c * P:(c + 1) * P], IDF[:, :])
                return mm

            def step(at, i, max_base, att_base, proj_base):
                def mine(name, l):
                    claim(pe, name, l, at, i)
                    return bank(name, l)

                def xt(l, new, part):
                    if l == 0:
                        pe.wait_ge(x_loaded, new * 16)
                    else:
                        pe.wait_ge(norm_done[l - 1], new)
                    transpose_tokens(X[l], mine("xt", l)).then_inc(xt_psum[l], 1)

                def ct(l, new, part):
                    pe.wait_ge(ctx_loaded, new * 16)
                    transpose_tokens(CTX, mine("ct", 1)).then_inc(ct_psum, 1)

                def feature_major(name, l, off, hi, lo, done):
                    dst = mine(name, l)
                    for t in range(C):
                        mm = three_pass(dst[:, t * TOK:(t + 1) * TOK],
                                        lambda c: WH[l][:, c, off + t * P:off + (t + 1) * P],
                                        lambda c: WL[l][:, c, off + t * P:off + (t + 1) * P],
                                        lambda c: hi[:, c, :], lambda c: lo[:, c, :])
                    mm.then_inc(done, 1)

                def q(l, new, part):
                    pe.wait_ge(xl_done[l], new)
                    feature_major("q", l, WQ, XH[l], XL[l], q_psum[l])

                def source(l):
                    return (CH, CL) if l == 1 else (XH[l], XL[l])

                def k(l, new, part):
                    if l == 1:
                        pe.wait_ge(cl_done, new)
                    feature_major("k", l, WK, *source(l), k_psum[l])

                def v(l, new, part):
                    hi, lo = source(l)
                    width = VG if l == 2 else D
                    for b in range(PB):
                        if l == 2:
                            dst, done = mine(("v", "v1")[b], l)[:, 0:width], v_psum[(l, b)]
                        else:
                            dst, done = (mine("v", l) if b == 0 else bank("v", l))[:, b * D:(b + 1) * D], v_psum[(l, 0)]
                        mm = three_pass(dst, lambda c: hi[:, c, b * P:(b + 1) * P], lambda c: lo[:, c, b * P:(b + 1) * P],
                                        lambda c: WH[l][:, c, WV:WV + width], lambda c: WL[l][:, c, WV:WV + width])
                        if l == 2 or b == 1:
                            mm.then_inc(done, 1)

                def head(stack, l, h, b):
                    return stack[l][:, h % HC, h // HC, b * P:(b + 1) * P]

                def row_max(l, new, p):
                    if p == 0:
                        for x in "qk":
                            pe.wait_ge(stacked[(x, l)], new * 16 * PARTS)
                    g = turn(MAX_ORDER, l, p, i)
                    if i != 0 or g >= 2:
                        pe.wait_ge(max_read, max_base + (g - 1))
                    dst = SM[g % 2]
                    for b in range(PB):
                        for h2 in range(2):
                            mm = pe.matmul(dst[:, b, h2, :], head(QS, l, 2 * p + h2, b), head(KS, l, 2 * p + h2, b),
                                           start=(b + h2 == 0), stop=(b + h2 == 2 and l == 2), skip_group_check=True)
                    if l < 2:
                        mm = pe.matmul(dst[:, :, :, :], IDB[:, :],
                                       MQ[l][:, :].unsqueeze(1).to_broadcast([P, 2 * PB, P]),
                                       start=False, stop=True, skip_group_check=True)
                    mm.then_inc(max_psum, 1)

                def max_t(l, new, part):
                    pe.wait_ge(nm_done[l], new)
                    dst = mine("maxt", l)
                    for b in range(PB):
                        mm = pe.transpose(dst[:, b * P // 2:(b + 1) * P // 2].bitcast(BF16),
                                          NMB[:, b, :, :, :].rearrange("p r k h -> p (r k h)"), IDB[:, :])
                    mm.then_inc(mt_psum[l], 1)

                def scores(l, p):
                    g = turn(ATT_ORDER, l, p, i)
                    if i != 0 or g >= 2:
                        pe.wait_ge(probs_done, att_base + (g - 1))
                    dst = SS[g % 2]
                    j = QUAD * (p % 4)
                    for b in range(PB):
                        for h2 in range(2):
                            pe.matmul(dst[:, b, h2, :], head(KS, l, 2 * p + h2, b), head(QS, l, 2 * p + h2, b),
                                      start=(b + h2 == 0), stop=False, skip_group_check=True)
                    if l < 2:
                        pe.matmul(dst[:, :, :, :], IDB[:, :],
                                  MK[l][:, :].unsqueeze(1).to_broadcast([P, 2 * PB, P]),
                                  start=False, stop=False, skip_group_check=True)
                    for h2 in range(2):
                        mm = pe.matmul(dst[:, :, h2, :], SEL[j:j + QUAD, 2 * p + h2:2 * p + h2 + 1].to_broadcast([QUAD, P]),
                                       MT[l][j:j + QUAD, :].rearrange("p (b q) -> p b q", b=PB),
                                       start=False, stop=(h2 == 1), tile_position=(j, 0), skip_group_check=True)
                    mm.then_inc(score_psum, 1)

                def values(l, p):
                    g = turn(ATT_ORDER, l, p, i)
                    dst = mine(f"pv{p // 4}", l) if p % 4 == 0 else bank(f"pv{p // 4}", l)
                    pe.wait_ge(probs_done, att_base + (g + 1))
                    for b in range(PB):
                        for h2 in range(2):
                            j = QUAD * (2 * b + h2)
                            mm = pe.matmul(dst[j:j + QUAD, (p % 4) * P:(p % 4 + 1) * P], VA[l][:, b, 2 * p + h2, :],
                                           PR[slot(ATT_ORDER, l, p, i, 3)][:, b, h2, :],
                                           start=True, stop=True, tile_position=(0, j))
                    mm.then_inc(pv_psum, 1)

                def attend(l, new, p):
                    if p == 0:
                        pe.wait_ge(mt_done[l], new)
                        for b in range(PB if l == 2 else 1):
                            pe.wait_ge(v_done[(l, b)], new)
                    if p < PAIRS:
                        scores(l, p)
                    if p > 0:
                        values(l, p - 1)

                def z_tokens(l, new, f):
                    pe.wait_ge(za_done[(l, f)], new)
                    dst = mine(f"z{f}", l)
                    for p in range(4):
                        mm = pe.transpose(dst[:, p * P:(p + 1) * P], ZA[f][:, p, :], IDF[:, :])
                    mm.then_inc(z_psum[(l, f)], 1)

                def z_transposed(l, new, part):
                    for f in range(2):
                        pe.wait_ge(z_done[(l, f)], new)
                    transpose_tokens(Z[l][:, :, :, :].rearrange("p b h d -> p b (h d)"),
                                     mine("zt", l)).then_inc(zt_psum[l], 1)

                def out_proj(l, new, part):
                    pe.wait_ge(zl_done[l], new)
                    dst = mine("out", l)
                    for b in range(PB):
                        mm = three_pass(dst[:, b * D:(b + 1) * D],
                                        lambda c: XH[l][:, c, b * P:(b + 1) * P],
                                        lambda c: XL[l][:, c, b * P:(b + 1) * P],
                                        lambda c: WH[l][:, c, WO:WO + D], lambda c: WL[l][:, c, WO:WO + D])
                    mm.then_inc(o_psum[l], 1)

                def gate_t(l, new, part):
                    pe.wait_ge(combine_done, new)
                    dst = mine("gate", 2)
                    for b in range(PB):
                        mm = pe.transpose(dst[0:QUAD, b * P:(b + 1) * P], CB[:, b, :], IDF[:, :])
                    mm.then_inc(gt_psum, 1)

                def expert_bias(l, new, part):
                    pe.wait_ge(gt_done, new)
                    dst = mine("bias", 2)
                    for b in range(PB):
                        mm = pe.matmul(dst[:, b * D:(b + 1) * D], CBT[0:E, b * P:(b + 1) * P], EB[:, :],
                                       start=True, stop=True)
                    mm.then_inc(eb_psum, 1)

                def experts(l, new, g):
                    b, o = g % PB, WE + (g // PB) * 2 * D
                    three_pass(mine(f"e{g}", 2)[:, :],
                               lambda c: XH[2][:, c, b * P:(b + 1) * P], lambda c: XL[2][:, c, b * P:(b + 1) * P],
                               lambda c: WH[2][:, c, o:o + 2 * D],
                               lambda c: WL[2][:, c, o:o + 2 * D]).then_inc(e_psum[g], 1)

                work = {"xt": xt, "ct": ct, "q": q, "k": k, "v": v, "max": row_max, "maxt": max_t,
                        "attend": attend, "z": z_tokens, "zt": z_transposed, "out": out_proj, "gate": gate_t,
                        "experts": experts, "bias": expert_bias}
                for kind, l, lag, part in UNITS:
                    if kind in work and active(i, lag):
                        work[kind](l, at[1 - lag], part)

            steps(pe, step)

        @block.scalar
        def _(act):
            for n, (l, c0, ncols, parts) in enumerate(pieces):
                act.wait_ge(stage_loaded[n % 3], staged[n])
                act.activation(WH[l][:, :, c0:c0 + ncols], stage(n, ncols), ACT.Copy).then_inc(w_hi_done, 1)
            act.wait_ge(setup_v, 3)

            def step(at, i, max_base, att_base, proj_base):
                def rounded(dst, src, ready, new, done):
                    act.wait_ge(ready, new)
                    act.activation(dst[:, :, :].rearrange("p c t -> p (c t)"), src[:, :], ACT.Copy).then_inc(done, 1)

                def xt(l, new, part):
                    rounded(XH[l], bank("xt", l), xt_psum[l], new, xh_done[l])

                def ct(l, new, part):
                    rounded(CH, bank("ct", 1), ct_psum, new, ch_done)

                def project(x, l):
                    n = proj_base + proj_turn(l, i)
                    full, parts, src = (QF, QP, bank("q", l)) if x == "q" else (KF, KP, bank("k", l))
                    if not (isinstance(n, int) and n == 1):
                        act.wait_ge(low_done[x], n - 1)
                    for t in range(C):
                        if x == "q":
                            ins = act.activation(full[:, t, :], src[:, t * TOK:(t + 1) * TOK], ACT.Identity,
                                                 bias=QBI[:, l, t:t + 1], scale=SCALE)
                        else:
                            ins = act.activation(full[:, t, :], src[:, t * TOK:(t + 1) * TOK], ACT.Identity,
                                                 bias=COLB[:, l, 1, t:t + 1])
                    return n, full, parts, ins

                def high(x, n, full, parts):
                    if not (isinstance(n, int) and n == 1):
                        act.wait_ge(stored[x], (n - 1) * 16 * PARTS)
                    act.activation(parts[:, 0, :, :], full[:, :, :], ACT.Copy).then_inc(hi_done[x], 1)

                def middle(x, l):
                    n = proj_base + proj_turn(l, i)
                    full, parts = (QF, QP) if x == "q" else (KF, KP)
                    act.wait_ge(rest_done[x], n)
                    act.activation(parts[:, 1, :, :], full[:, :, :], ACT.Copy).then_inc(mid_done[x], 1)

                def q(l, new, part):
                    act.wait_ge(q_psum[l], new)
                    n, full, parts, ins = project("q", l)
                    ins.then_inc(qf_done[l], 1)
                    act.wait_ge(qf_done[l], new)
                    high("q", n, full, parts)

                def k(l, new, part):
                    act.wait_ge(k_psum[l], new)
                    n, full, parts, ins = project("k", l)
                    ins.then_inc(kf_done[l], 1)
                    act.wait_ge(kf_done[l], new)
                    high("k", n, full, parts)
                    middle("q", l)

                def v(l, new, part):
                    middle("k", l)
                    if l == 2:
                        act.wait_ge(gate_max, new)
                        for b in range(PB):
                            ins = act.activation(GE[:, b, :], GL[:, b, :], ACT.Exp, bias=GN[:, b:b + 1],
                                                 accum_out=GS[:, b:b + 1])
                        ins.then_inc(gate_exp, 1)

                def max_t(l, new, part):
                    act.wait_ge(mt_psum[l], new)
                    act.activation(MT[l][:, :], bank("maxt", l)[:, 0:P].bitcast(BF16), ACT.Copy).then_inc(mt_done[l], 1)

                def z_half(l, f):
                    act.wait_ge(pv_psum, att_base + (turn(ATT_ORDER, l, 4 * f + 3, i) + 1))
                    act.activation(ZA[f][:, :, :].rearrange("p k q -> p (k q)"), bank(f"pv{f}", l)[:, :],
                                   ACT.Copy).then_inc(za_done[(l, f)], 1)

                def attend(l, new, p):
                    if p in (5, 8):
                        z_half(l, p // 8)
                    if p == PAIRS:
                        return
                    g = turn(ATT_ORDER, l, p, i)
                    act.wait_ge(score_psum, att_base + (g + 1))
                    if i != 0 or g >= 3:
                        act.wait_ge(pv_psum, att_base + (g - 2))
                    act.activation(PR[slot(ATT_ORDER, l, p, i, 3)][:, :, :, :], SS[g % 2][:, :, :, :],
                                   ACT.Exp).then_inc(probs_done, 1)

                def z_transposed(l, new, part):
                    rounded(XH[l], bank("zt", l), zt_psum[l], new, zh_done[l])

                work = {"xt": xt, "ct": ct, "q": q, "k": k, "v": v, "maxt": max_t, "attend": attend,
                        "zt": z_transposed}
                for kind, l, lag, part in UNITS:
                    if kind in work and active(i, lag):
                        work[kind](l, at[1 - lag], part)

            steps(act, step)

        @block.vector
        def _(dve):
            own = [0]

            def setup_link(ins):
                own[0] += 1
                ins.then_inc(dve_setup, 1)
                dve.wait_ge(dve_setup, own[0])

            dve.wait_ge(const_loaded, CONSTS_LOADED)
            dve.tensor_copy(IDF[:, :], CONST[:, 0:P])
            dve.tensor_copy(IDB[:, :], CONST[:, 0:P])
            dve.tensor_scalar(MQ[0][:, :], CONST[:, P:2 * P], -MASKED, MASKED, ALU.mult, ALU.add)
            setup_link(dve.tensor_copy(MF[:, :], MI[:, :]))
            setup_link(dve.tensor_scalar(MQ[1][:, :], MF[:, :], 0.0, MASKED, ALU.is_equal, ALU.mult))
            dve.tensor_copy(SEL[:, :], CONST[:, 2 * P:2 * P + H])
            setup_link(dve.tensor_scalar(QBI[:, :, :], COLB[:, :, 0, :], SCALE, None, ALU.mult))
            dve.memset(NHALF[:, :], -0.5)
            dve.memset(EPSC[:, :], EPS)
            setup_link(dve.memset(CB[:, :, :], 0.0))
            dve.memset(GN[:, :], 0.0).then_inc(setup_v, 1)
            for j in range(2):
                dve.wait_ge(setup_pe, j + 1)
                dve.tensor_copy(MK[j][:, :], WB[j][:, 0:P // 2].bitcast(BF16)).then_inc(setup_v, 1)
            for n, (l, c0, ncols, parts) in enumerate(pieces):
                dve.wait_ge(w_hi_done, n + 1)
                dve.tensor_tensor(WL[l][:, :, c0:c0 + ncols], stage(n, ncols),
                                  WH[l][:, :, c0:c0 + ncols].bitcast(F32), ALU.subtract).then_inc(w_lo_done, 1)
            dve.wait_ge(setup_p, 1)
            IOTA = CONST[:, 2 * P + H:2 * P + H + E]

            def step(at, i, max_base, att_base, proj_base):
                def carry(s, value):
                    dve.wait_ge(s, value)
                    dve.memset(SPARE[:, :], 0.0)

                per = sum(links(kind, l, part) for kind, l, _, part in UNITS)
                linked = [link_base(i) if i is not None else dve.snap(at[0] * per - (per * (DEPTH + 1) - link_base(DEPTH + 1))), 0]

                def link(ins, carried=False):
                    linked[1] += 1
                    ins.then_inc(vector_link, 1)
                    if carried:
                        carry(vector_link, linked[0] + linked[1])
                    else:
                        dve.wait_ge(vector_link, linked[0] + linked[1])

                def flat(t):
                    return t[:, :, :].rearrange("p c t -> p (c t)")

                def low(dst, src, hi, ready, new, done):
                    dve.wait_ge(ready, new)
                    dve.tensor_tensor(flat(dst), src[:, :], flat(hi).bitcast(F32), ALU.subtract).then_inc(done, 1)

                def xt(l, new, part):
                    low(XL[l], bank("xt", l), XH[l], xh_done[l], new, xl_done[l])

                def ct(l, new, part):
                    low(CL, bank("ct", 1), CH, ch_done, new, cl_done)

                def v(l, new, part):
                    for b in range(PB):
                        if l == 2:
                            dve.wait_ge(v_psum[(l, b)], new)
                            src = bank(("v", "v1")[b], l)
                            dve.tensor_tensor(GL[:, b, :], src[:, D:VG], RB[:, RB_V[2] + D:RB_V[2] + VG], ALU.add)
                            o = 0
                        else:
                            if b == 0:
                                dve.wait_ge(v_psum[(l, 0)], new)
                            src = bank("v", l)
                            o = b * D
                        ins = dve.tensor_tensor(VA[l][:, b, :, 0:DH],
                                                src[:, o:o + D].rearrange("p (h d) -> p h d", h=H),
                                                RB[:, RB_V[l]:RB_V[l] + D].rearrange("p (h d) -> p h d", h=H), ALU.add)
                        if l == 2:
                            ins.then_inc(v_done[(l, b)], 1)
                    if l < 2:
                        ins.then_inc(v_done[(l, 0)], 1)
                    else:
                        dve.wait_ge(v_done[(2, 1)], new)
                        dve.tensor_reduce(GN[:, :], GL[:, :, :], AX.X, ALU.max, negate=True).then_inc(gate_max, 1)

                def gate_top(n):
                    dve.wait_ge(gate_exp, n)
                    link(dve.reciprocal(GR[:, :], GS[:, :]))
                    for b in range(PB):
                        ins = dve.tensor_scalar(GP[:, b, :], GE[:, b, :], GR[:, b:b + 1], None, ALU.mult)
                    link(ins, carried=True)
                    for b in range(PB):
                        ins = dve.max(GT[:, b, :], GP[:, b, :])
                    link(ins, carried=True)
                    for b in range(PB):
                        ins = dve.max_index(GI[:, b, :], GT[:, b, :], GP[:, b, :])
                    link(ins)
                    link(dve.tensor_copy(GF[:, :, :], GI[:, :, :]))
                    for b in range(PB):
                        dve.tensor_scalar(G1[:, b, :], IOTA, GF[:, b, 0:1], GT[:, b, 0:1], ALU.is_equal, ALU.mult)
                        ins = dve.tensor_scalar(G2[:, b, :], IOTA, GF[:, b, 1:2], GT[:, b, 1:2], ALU.is_equal,
                                                ALU.mult)
                    link(ins)
                    dve.tensor_tensor(CB[:, :, 0:E], G1[:, :, :], G2[:, :, :], ALU.add).then_inc(combine_done, 1)

                def row_max(l, new, p):
                    g = turn(MAX_ORDER, l, p, i)
                    dve.wait_ge(max_psum, max_base + (g + 1))
                    dve.tensor_reduce(NM[:, :, 2 * p:2 * p + 2], SM[g % 2][:, :, :, :], AX.X, ALU.max,
                                      negate=True).then_inc(max_read, 1)
                    if l == 2 and p == 1:
                        gate_top(new)
                    if p < PAIRS - 1:
                        return
                    m, val = before(MAX_ORDER, l, at, i)
                    if m is not None:
                        dve.wait_ge(mt_psum[m], val)
                    dve.wait_ge(max_read, max_base + (g + 1))
                    for b in range(PB):
                        ins = dve.tensor_copy(NMB[:, b, :, 0, :], NM[:, b, :].unsqueeze(1).to_broadcast([P, 4, H]))
                    link(ins)
                    for b in range(PB):
                        ins = dve.tensor_tensor(NMB[:, b, :, 1, :], NM[:, b, :].unsqueeze(1).to_broadcast([P, 4, H]),
                                                NMB[:, b, :, 0, :], ALU.subtract)
                    ins.then_inc(nm_done[l], 1)

                def z_tokens(l, new, f):
                    dve.wait_ge(z_psum[(l, f)], new)
                    src = bank(f"z{f}", l)[:, :].rearrange("q (p b h d) -> q p b h d", p=4, b=PB, h=2)
                    rz = RZ[:, :, 4 * f:4 * f + 4, :]
                    for b in range(PB):
                        ins = dve.reciprocal(rz[:, b, :, :].unsqueeze(3), src[:, :, b, :, DH:DH + 1])
                    link(ins)
                    for b in range(PB):
                        ins = dve.tensor_tensor(Z[l][:, b, 8 * f:8 * f + 8, :].rearrange("q (p h) d -> q p h d", p=4),
                                                src[:, :, b, :, 0:DH],
                                                rz[:, b, :, :].unsqueeze(3).to_broadcast([P, 4, 2, DH]), ALU.mult)
                    ins.then_inc(z_done[(l, f)], 1)

                def z_transposed(l, new, part):
                    low(XL[l], bank("zt", l), XH[l], zh_done[l], new, zl_done[l])

                def normalise(l, lag):
                    new, old = at[1 - lag], at[-lag]
                    for b in range(PB):
                        ins = dve.bn_stats(ST[:, l, b, :], XB[l][:, b, :])
                    link(ins, carried=True)
                    for b in range(PB):
                        ins = dve.bn_aggr(MV[:, l, b, :], ST[:, l, b, :])
                    ins.then_inc(mv_done[l], 1)
                    dst = X[l + 1] if l < 2 else XB[2]
                    if l < 2 and (i is None or i > lag):
                        dve.wait_ge(xb_done[1] if l == 0 else eb_done, old)
                        dve.wait_ge(xt_psum[l + 1], old)
                    dve.wait_ge(rs_done[l], new)
                    for b in range(PB):
                        ins = dve.tensor_scalar(dst[:, b, :], XB[l][:, b, :], MV[:, l, b, 0:1], RS[:, l, b:b + 1],
                                                ALU.subtract, ALU.mult)
                    ins.then_inc(norm_done[l], 1)

                def out_proj(l, new, lag):
                    dve.wait_ge(o_psum[l], new)
                    dve.wait_ge(xb_done[l], new)
                    xb = XB[l][:, :, :].rearrange("p b d -> p (b d)")
                    dve.tensor_tensor(xb, bank("out", l)[:, :], xb, ALU.add).then_inc(sum_done[l], 1)
                    dve.wait_ge(sum_done[l], new)
                    normalise(l, lag)

                def gate_t(l, new, part):
                    dve.wait_ge(gt_psum, new)
                    dve.tensor_copy(CBT[:, :], bank("gate", 2)[0:QUAD, 0:TOK]).then_inc(gt_done, 1)

                def expert_bias(l, new, lag):
                    if i is None or i > lag:
                        dve.wait_ge(out_stored, at[-lag] * 16)
                    dve.wait_ge(eb_psum, new)
                    dve.tensor_tensor(XB[2][:, :, :].rearrange("p b d -> p (b d)"), bank("bias", 2)[:, :],
                                      X[2][:, :, :].rearrange("p b d -> p (b d)"), ALU.add).then_inc(eb_done, 1)

                def experts(l, new, g):
                    b, acc = g % PB, XB[2]
                    dve.wait_ge(e_psum[g], new)
                    for half in range(2):
                        e = 2 * (g // PB) + half
                        if half:
                            dve.wait_ge(e_half[g], new)
                        elif g < PB:
                            dve.wait_ge(eb_done, new)
                        else:
                            dve.wait_ge(e_done[g - PB], new)
                        dve.scalar_tensor_tensor(
                            out=acc[:, b, :], in0=bank(f"e{g}", 2)[:, half * D:(half + 1) * D],
                            scalar=CB[:, b, e:e + 1], in1=acc[:, b, :], op0=ALU.mult,
                            op1=ALU.add).then_inc((e_done if half else e_half)[g], 1)

                def finish(l, new, lag):
                    for g in range(E - PB, E):
                        dve.wait_ge(e_done[g], new)
                    dve.tensor_tensor(XB[2][:, :, :], XB[2][:, :, :],
                                      Z[2][:, :, :, :].rearrange("p b h d -> p b (h d)"),
                                      ALU.add).then_inc(sum_done[2], 1)
                    dve.wait_ge(sum_done[2], new)
                    normalise(2, lag)

                work = {"xt": xt, "ct": ct, "v": v, "max": row_max, "z": z_tokens,
                        "zt": z_transposed, "out": out_proj, "gate": gate_t, "experts": experts, "finish": finish,
                        "bias": expert_bias}
                for kind, l, lag, part in UNITS:
                    if kind in work and active(i, lag):
                        work[kind](l, at[1 - lag], lag if kind in ("out", "finish", "bias") else part)

            steps(dve, step)

        @block.gpsimd
        def _(pool):
            pool.wait_ge(w_lo_done, len(pieces))
            for l in range(NL):
                ins = pool.memset(VA[l][:, :, :, DH:QUAD], 1.0)
            ins.then_inc(setup_p, 1)
            pool.wait_ge(setup_v, 1)

            def step(at, i, max_base, att_base, proj_base):
                def residual(l, lag):
                    new = at[1 - lag]
                    if l == 0:
                        pool.wait_ge(x_loaded, new * 16)
                    else:
                        pool.wait_ge(norm_done[l - 1], new)
                    if i is None or i > lag:
                        pool.wait_ge(norm_done[l], at[-lag])
                    for b in range(PB):
                        ins = pool.tensor_tensor(XB[l][:, b, :], X[l][:, b, :], RB[:, RB_O[l]:RB_O[l] + D], ALU.add)
                    ins.then_inc(xb_done[l], 1)

                def rstd(l, lag):
                    new = at[1 - lag]
                    pool.wait_ge(mv_done[l], new)
                    pool.tensor_tensor(VE[:, l, :], MV[:, l, :, 1], EPSC[:, :], ALU.add).then_inc(ve_done[l], 1)
                    pool.wait_ge(ve_done[l], new)
                    pool.tensor_tensor(RS[:, l, :], VE[:, l, :], NHALF[:, :], ALU.pow).then_inc(rs_done[l], 1)

                def rest(x, l):
                    n = proj_base + proj_turn(l, i)
                    full, parts = (QF, QP) if x == "q" else (KF, KP)
                    pool.wait_ge(hi_done[x], n)
                    pool.tensor_tensor(full[:, :, :], full[:, :, :], parts[:, 0, :, :], ALU.subtract).then_inc(rest_done[x], 1)

                def lowest(x, l):
                    n = proj_base + proj_turn(l, i)
                    full, parts = (QF, QP) if x == "q" else (KF, KP)
                    pool.wait_ge(mid_done[x], n)
                    pool.tensor_tensor(parts[:, 2, :, :], full[:, :, :], parts[:, 1, :, :], ALU.subtract).then_inc(low_done[x], 1)

                for kind, l, lag, part in UNITS:
                    if active(i, lag):
                        if kind == "q":
                            rest("q", l)
                        if kind == "k":
                            rest("k", l)
                            lowest("q", l)
                        if kind == "v":
                            lowest("k", l)
                        if kind == "xt" and l < 2:
                            residual(l, lag)
                        if kind in ("out", "finish"):
                            rstd(l, lag)

            steps(pool, step)


def kernel(x, ctx_1024, mask_1x1xSxS2_ik0, L0_attn_W_qkv, L0_attn_b_qkv, L0_attn_W_proj, L0_attn_b_proj,
           L0_xattn_wq, L0_xattn_bq, L0_xattn_wk, L0_xattn_bk, L0_xattn_wv, L0_xattn_bv, L0_xattn_wo, L0_xattn_bo,
           L0_ffn_W_qkv, L0_ffn_b_qkv, L0_ffn_W_gate, L0_ffn_b_gate, L0_ffn_W_experts, L0_ffn_b_experts):
    import numpy as np
    import concourse.bacc as bacc
    from concourse.bass_utils import run_bass_kernel_spmd

    def a(v):
        return np.asarray(v)

    part = np.arange(P)
    consts = np.concatenate([
        np.eye(P), np.tril(np.ones((P, P))), part[:, None] % H == np.arange(H)[None, :],
        np.tile(np.arange(E), (P, 1)),
    ], axis=1).astype(np.float32)
    row = np.concatenate([a(L0_attn_b_qkv)[2 * D:], a(L0_attn_b_proj), a(L0_xattn_bv), a(L0_xattn_bo),
                          a(L0_ffn_b_qkv)[2 * D:], a(L0_ffn_b_gate)])
    rows = np.ascontiguousarray(np.broadcast_to(row[None, :], (P, RB_COLS)))
    col = np.stack([a(L0_attn_b_qkv)[:2 * D], np.concatenate([a(L0_xattn_bq), a(L0_xattn_bk)]),
                    a(L0_ffn_b_qkv)[:2 * D]])
    cols = np.ascontiguousarray(col.reshape(NL * 2 * C, P).T)
    arrays = {
        "x": a(x), "ctx": a(ctx_1024), "mask": np.ascontiguousarray(a(mask_1x1xSxS2_ik0).reshape(P, P)),
        "qkv0": a(L0_attn_W_qkv), "o0": a(L0_attn_W_proj),
        "q1": np.ascontiguousarray(a(L0_xattn_wq).T), "k1": np.ascontiguousarray(a(L0_xattn_wk).T),
        "v1": np.ascontiguousarray(a(L0_xattn_wv).T), "o1": np.ascontiguousarray(a(L0_xattn_wo).T),
        "qkv2": a(L0_ffn_W_qkv), "gate": a(L0_ffn_W_gate), "experts": a(L0_ffn_W_experts),
        "eb": a(L0_ffn_b_experts), "rows": rows, "cols": cols, "consts": consts,
    }
    nc = bacc.Bacc("TRN2", target_bir_lowering=False, num_devices=1)
    t = {n: nc.dram_tensor(f"in_{n}", v.shape, mybir.dt.from_np(v.dtype), kind="ExternalInput").ap()
         for n, v in arrays.items()}
    out = nc.dram_tensor("out_0", (B, P, D), F32, kind="ExternalOutput").ap()
    split = {x: nc.dram_tensor(f"{x}_split", (HC, PARTS, DH, C * TOK), BF16, kind="Internal").ap() for x in "qk"}
    decoder(nc, t["x"], t["ctx"], t["mask"], t, t["rows"], t["cols"], t["eb"], t["consts"], split, out)
    r = run_bass_kernel_spmd(nc, [{f"in_{n}": v for n, v in arrays.items()}], core_ids=[0])
    return r.results[0]["out_0"]
```

```python
from contextlib import ExitStack

import concourse.bass as bass
from concourse import mybir
from concourse.alu_op_type import AluOpType as ALU

ACT = mybir.ActivationFunctionType
F32 = mybir.dt.float32
F32R = mybir.dt.float32r
BF16 = mybir.dt.bfloat16
U32 = mybir.dt.uint32
AX = mybir.AxisListType

P = 128
D = 256
H = 16
DH = D // H
E = 8
B = 32
PB = 2
TOK = PB * P
NSTEP = B // PB
NL = 3
C = D // P
QUAD = 32
SCALE = DH ** -0.5
EPS = 1e-5
MASKED = -(2.0 ** 100)
STAGES = 4
PARTS = 3
HC = P // DH
STACK_FROM = {"q": [(0, 3), (0, 2), (0, 1)], "k": [(0, 3), (1, 3), (2, 3)]}
PLACE = {"q": [0, 1, 2], "k": [2, 1, 0]}
MAX_PARTS = 2
ROWS = DH * sum(b - a for a, b in STACK_FROM["q"])
VG = D + E

WQ, WK, WV, WO = 0, D, 2 * D, 3 * D
WE = 2 * D + VG
WCOLS = [4 * D, 4 * D, WE + E * D]
RB_V = [0, 2 * D, 4 * D]
RB_O = [D, 3 * D]
RB_COLS = 4 * D + VG

PAIRS = H // 2
STEP_TICKS = 24
LAYER_TIMES = [
    {"xt": [1.74], "q": [2.95], "qmid": [3.97], "k": [4.3], "kmid": [5.13], "v": [6.59], "stack": [7.46],
     "max": [10.1, 10.63, 11.16, 11.69, 12.22, 12.75, 13.28, 13.8], "maxt": [13.97], "maxload": [14.32],
     "attend": [16.05, 17.02, 17.99, 18.96, 19.93, 20.9, 21.87, 22.84, 23.81], "z": [23.91, 24.05],
     "zt": [25.56], "out": [26.61], "norm": [27.11]},
    {"xt": [31.93], "ct": [32.6], "q": [33.68], "qmid": [35.36], "k": [35.38], "kmid": [35.92],
     "v": [36.68], "stack": [37.79], "max": [40.53, 41.06, 41.59, 42.12, 42.65, 43.18, 43.71, 44.24],
     "maxt": [45.4], "maxload": [45.63],
     "attend": [48.05, 49.02, 49.99, 50.96, 51.93, 52.9, 53.87, 54.84, 55.81], "z": [55.14, 56.26],
     "zt": [56.99], "out": [58.68], "norm": [58.89]},
    {"xt": [65.98], "q": [66.95], "k": [67.55], "qmid": [67.8], "kmid": [68.2], "v": [68.61],
     "gexp": [68.68], "stack": [69.54], "max": [72.39, 72.88, 73.38, 73.87, 74.36, 74.85, 75.34, 75.84],
     "gate": [73.88], "bias": [75.05], "experts": [76.86, 77.3, 80.04, 80.33, 84.14, 84.83, 86.84, 87.01],
     "maxt": [76.93], "maxload": [78.41],
     "attend": [80.05, 81.02, 81.99, 82.96, 83.93, 84.9, 85.87, 86.84, 87.81], "z": [87.81, 88.35],
     "finish": [90.28], "norm": [90.8], "store": [91.0]},
]
TIMETABLE = sorted((t % STEP_TICKS, l, kind, int(t // STEP_TICKS), part)
                   for l in range(NL) for kind, times in LAYER_TIMES[l].items() for part, t in enumerate(times))
UNITS = [(kind, l, lag, part) for _, l, kind, lag, part in TIMETABLE]
DEPTH = max(u[2] for u in UNITS)
PROJ_ORDER = [u[1:3] for u in UNITS if u[0] == "q"]
MAX_ORDER = [u[1:3] for u in UNITS if u[0] == "max" and u[3] == 0]
ATT_ORDER = [u[1:3] for u in UNITS if u[0] == "attend" and u[3] == 0]
WORK_BANKS = 4


def work_uses():
    uses = []
    for kind, l, lag, part in UNITS:
        if kind in ("xt", "ct", "q", "k", "v", "maxt", "gate", "bias", "zt", "out"):
            uses.append((kind, l, lag))
        if kind == "v" and l == 2:
            uses.append(("v1", l, lag))
        if kind == "attend" and part in (1, 5):
            uses.append((f"pv{part // 4}", l, lag))
        if kind == "z":
            uses.append((f"z{part}", l, lag))
        if kind == "experts":
            uses.append((f"e{part}", 2, lag))
    return uses


USES = work_uses()
BANK_OF = {}
for _use in USES:
    BANK_OF[_use[:2]] = 0 if _use[0].startswith("pv") else 1 + sum(v > 0 for v in BANK_OF.values()) % (WORK_BANKS - 1)
assert len(BANK_OF) == len(USES)


def active(i, lag):
    return i is None or 0 <= i - lag < NSTEP


def decoder(nc, x, ctx, mask, w, rows, cols, eb, consts, split, out):
    with ExitStack() as stack:
        def sb(name, shape, dt=F32):
            return stack.enter_context(nc.sbuf_tensor(name, shape, dt))

        def sem(name):
            return stack.enter_context(nc.semaphore(name))

        def per_layer(name, layers=range(NL)):
            return {l: sem(f"{name}_{l}") for l in layers}

        def bufs(name, shape, dt=F32, n=NL):
            return [sb(f"{name}{l}", shape, dt) for l in range(n)]

        X = bufs("x", [P, PB, D])
        XB = bufs("res", [P, PB, D])
        CTX = sb("ctx", [P, PB, D])
        XH = bufs("x_hi", [P, C, TOK], F32R)
        XL = bufs("x_lo", [P, C, TOK], F32R)
        ZH = sb("z_hi", [P, C, TOK], F32R)
        ZL = sb("z_lo", [P, C, TOK], F32R)
        CH = sb("c_hi", [P, C, TOK], F32R)
        CL = sb("c_lo", [P, C, TOK], F32R)
        QF = sb("q_full", [P, C, TOK])
        KF = sb("k_full", [P, C, TOK])
        QP = sb("q_parts", [P, PARTS, C, TOK], BF16)
        KP = sb("k_parts", [P, PARTS, C, TOK], BF16)
        QS = bufs("q_stack", [P, HC, C, TOK], BF16)
        KS = bufs("k_stack", [P, HC, C, TOK], BF16)
        VA = bufs("v_ones", [P, PB, H, QUAD])
        NM = sb("neg_max", [P, PB, H])
        NMB = sb("neg_max_parts", [P, PB, MAX_PARTS, HC, C], BF16)
        MT = bufs("neg_max_t", [MAX_PARTS * H, TOK], BF16)
        PR = bufs("probs", [P, PB, 2, P], F32, 3)
        ZA = bufs("z_aug", [P, 4, P], F32, 2)
        Z = bufs("z", [P, PB, H, DH], n=2)
        RZ = sb("z_recip", [P, PB, PAIRS, 2])
        ST = sb("bn_stats", [P, NL, PB, 6])
        MV = sb("mean_var", [P, NL, PB, 2])
        VE = sb("var_eps", [P, NL, PB])
        RS = sb("rstd", [P, NL, PB])
        GL = sb("gate_logits", [P, PB, E])
        GN = sb("gate_neg_max", [P, PB])
        GE = sb("gate_exp", [P, PB, E])
        GS = sb("gate_sum", [P, PB])
        GR = sb("gate_recip", [P, PB])
        GP = sb("gate_probs", [P, PB, E])
        GT = sb("gate_top", [P, PB, 8])
        GI = sb("gate_index", [P, PB, 8], U32)
        GF = sb("gate_index_f", [P, PB, 8])
        G1 = sb("combine_first", [P, PB, E])
        G2 = sb("combine_second", [P, PB, E])
        CB = sb("combine", [P, PB, QUAD])
        CBT = sb("combine_t", [QUAD, TOK])
        WH = [sb(f"w_hi{l}", [P, C, WCOLS[l]], F32R) for l in range(NL)]
        WL = [sb(f"w_lo{l}", [P, C, WCOLS[l]], F32R) for l in range(NL)]
        IDB = sb("ident_b", [P, P], BF16)
        CONST = sb("consts", [P, P + P + E])
        IDF = CONST[:, 0:P]
        MI = sb("mask_int", [P, P], mybir.dt.int32)
        MF = sb("mask_f", [P, P])
        MQ = bufs("mask_qk", [P, P], BF16, 2)
        MK = bufs("mask_kq", [P, P], BF16, 2)
        RB = sb("row_bias", [P, RB_COLS])
        COLB = sb("col_bias", [P, NL, 2, C])
        QBI = sb("q_bias_scaled", [P, NL, C])
        EB = sb("expert_bias", [E, D])
        NHALF = sb("minus_half", [P, PB])
        EPSC = sb("epsilon", [P, PB])
        SPARE = sb("spare", [P, 1])

        SM = [stack.enter_context(nc.psum_tensor(f"max_scores{i}", [P, PB, 2, P], F32)) for i in range(2)]
        SS = [stack.enter_context(nc.psum_tensor(f"scores{i}", [P, PB, 2, P], F32)) for i in range(2)]
        WB = [stack.enter_context(nc.psum_tensor(f"work{i}", [P, 512], F32)) for i in range(WORK_BANKS)]

        def bank(name, l):
            return WB[BANK_OF[(name, l)]]

        const_loaded = sem("const_loaded")
        stage_loaded = [sem(f"stage_loaded{n}") for n in range(STAGES)]
        w_hi_done = sem("w_hi_done")
        w_lo_done = sem("w_lo_done")
        setup_v = sem("setup_v")
        setup_pe = sem("setup_pe")
        setup_p = sem("setup_p")
        dve_setup = sem("dve_setup")
        x_loaded = sem("x_loaded")
        ctx_loaded = sem("ctx_loaded")
        out_stored = sem("out_stored")
        xt_psum = per_layer("xt_psum")
        xh_done = per_layer("xh_done")
        xl_done = per_layer("xl_done")
        xb_done = per_layer("xb_done", (0, 1))
        ct_psum, ch_done, cl_done = sem("ct_psum"), sem("ch_done"), sem("cl_done")
        q_psum = per_layer("q_psum")
        k_psum = per_layer("k_psum")
        v_psum = {(l, b): sem(f"v_psum_{l}{b}") for l, b in ((0, 0), (1, 0), (2, 0), (2, 1))}
        v_done = {(l, b): sem(f"v_done_{l}{b}") for l, b in ((0, 0), (1, 0), (2, 0), (2, 1))}
        qf_done = per_layer("qf_done")
        kf_done = per_layer("kf_done")
        nm_done = per_layer("nm_done")
        mt_psum = per_layer("mt_psum")
        mt_done = per_layer("mt_done")
        max_stacked = per_layer("max_stacked")
        za_done = {(l, f): sem(f"za_done_{l}{f}") for l in range(NL) for f in range(2)}
        z_psum = {(l, f): sem(f"z_psum_{l}{f}") for l in range(NL) for f in range(2)}
        z_done = {(l, f): sem(f"z_done_{l}{f}") for l in range(NL) for f in range(2)}
        zt_psum = per_layer("zt_psum", (0, 1))
        zh_done = per_layer("zh_done", (0, 1))
        zl_done = per_layer("zl_done", (0, 1))
        o_psum = per_layer("o_psum", (0, 1))
        sum_done = per_layer("sum_done")
        mv_done = per_layer("mv_done")
        ve_done = per_layer("ve_done")
        rs_done = per_layer("rs_done")
        norm_done = per_layer("norm_done")
        max_psum = sem("max_psum")
        max_read = sem("max_read")
        score_psum = sem("score_psum")
        probs_done = sem("probs_done")
        pv_psum = sem("pv_psum")
        hi_done, rest_done, mid_done, low_done, stored = (
            {x: sem(f"{x}_{name}") for x in "qk"} for name in ("hi", "rest", "mid", "low", "stored"))
        stacked = {(x, l): sem(f"{x}_stacked_{l}") for x in "qk" for l in range(NL)}
        vector_link = sem("vector_link")
        gate_max, gate_exp, combine_done = sem("gate_max"), sem("gate_exp"), sem("combine_done")
        gt_psum, gt_done, eb_psum, eb_done = sem("gt_psum"), sem("gt_done"), sem("eb_psum"), sem("eb_done")
        e_psum = [sem(f"e_psum_{g}") for g in range(E)]
        e_half = [sem(f"e_half_{g}") for g in range(E)]
        e_done = [sem(f"e_done_{g}") for g in range(E)]

        read_by = {}
        for l in range(NL):
            read_by[("xt", l)] = xl_done[l]
            read_by[("q", l)] = qf_done[l]
            read_by[("k", l)] = kf_done[l]
            read_by[("v", l)] = v_done[(l, 0)]
            read_by[("maxt", l)] = mt_done[l]
            for f in range(2):
                read_by[(f"pv{f}", l)] = za_done[(l, f)]
                read_by[(f"z{f}", l)] = z_done[(l, f)]
        for l in (0, 1):
            read_by[("zt", l)] = zl_done[l]
            read_by[("out", l)] = sum_done[l]
        read_by[("ct", 1)] = cl_done
        read_by[("v1", 2)] = v_done[(2, 1)]
        read_by[("gate", 2)] = gt_done
        read_by[("bias", 2)] = eb_done
        for g in range(E):
            read_by[(f"e{g}", 2)] = e_done[g]

        def steps(eng, body, end=NSTEP, prepare=lambda l: None):
            def straight(i):
                body({c: i + c for c in range(-DEPTH, 2)}, i, ring_base(MAX_ORDER, i), ring_base(ATT_ORDER, i),
                     ring_base(PROJ_ORDER, i) // PAIRS)
            full = DEPTH + 1
            for i in range(full):
                if i < NL:
                    prepare(i)
                straight(i)
            with eng.Fori(full, end) as i:
                at = {c: eng.snap(i + c) for c in range(-DEPTH, 2)}
                per = NL * PAIRS
                body(at, None, eng.snap(i * per - (per * full - ring_base(MAX_ORDER, full))),
                     eng.snap(i * per - (per * full - ring_base(ATT_ORDER, full))),
                     eng.snap(i * NL - (NL * full - ring_base(PROJ_ORDER, full) // PAIRS)))
            for i in range(end, NSTEP + DEPTH):
                straight(i)

        def ring_base(order, i):
            return PAIRS * sum(active(j, lag) for j in range(i) for _, lag in order)

        def links(kind, l, part):
            return {"z": 1, "out": 1, "finish": 1}.get(kind, 0) + (kind == "max") * ((part == PAIRS - 1) + 6 * (l == 2 and part == 1))

        def link_base(i):
            return sum(links(kind, l, part) for j in range(i) for kind, l, lag, part in UNITS if active(j, lag))

        def turn(order, l, p, i):
            return PAIRS * [m for m, lag in order if active(i, lag)].index(l) + p

        def proj_turn(l, i):
            return turn(PROJ_ORDER, l, 0, i) // PAIRS + 1

        def slot(order, l, p, i, n):
            return (ring_base(order, DEPTH + 1 if i is None else i) + turn(order, l, p, i)) % n

        def before(order, l, at, i):
            n = [m for m, _ in order].index(l)
            for m, lag in reversed(order[:n]):
                if active(i, lag):
                    return m, at[1 - lag]
            for m, lag in reversed(order):
                if active(i if i is None else i - 1, lag):
                    return m, at[-lag]
            return None, None

        def claim(eng, name, l, at, i):
            mine, uses = BANK_OF[(name, l)], [u[:2] for u in USES]
            here = uses.index((name, l))
            for use in reversed(USES[:here]):
                if BANK_OF[use[:2]] == mine and active(i, use[2]):
                    return eng.wait_ge(read_by[use[:2]], at[1 - use[2]])
            for use in reversed(USES):
                if BANK_OF[use[:2]] == mine and active(i if i is None else i - 1, use[2]):
                    return eng.wait_ge(read_by[use[:2]], at[-use[2]])

        x_v = x.rearrange("(n b) s d -> n s b d", b=PB)
        ctx_v = ctx.rearrange("(n b) s d -> n s b d", b=PB)
        out_v = out.rearrange("(n b) s d -> n s b d", b=PB)

        def cols_of(ap, a, b):
            return ap.rearrange("(c p) n -> p c n", p=P)[:, :, a:b]

        pieces = [
            (0, WQ, 2 * D, [(0, cols_of(w["qkv0"], 0, 2 * D))]),
            (0, WV, 2 * D, [(0, cols_of(w["qkv0"], 2 * D, 3 * D)), (D, cols_of(w["o0"], 0, D))]),
            (1, WQ, 2 * D, [(0, cols_of(w["q1"], 0, D)), (D, cols_of(w["k1"], 0, D))]),
            (1, WV, 2 * D, [(0, cols_of(w["v1"], 0, D)), (D, cols_of(w["o1"], 0, D))]),
            (2, WQ, 2 * D, [(0, cols_of(w["qkv2"], 0, 2 * D))]),
            (2, WV, VG, [(0, cols_of(w["qkv2"], 2 * D, 3 * D)), (D, cols_of(w["gate"], 0, E))]),
        ]
        for g in range(E // 2):
            pieces.append((2, WE + 2 * g * D, 2 * D,
                           [(j * D, cols_of(w["experts"][2 * g + j], 0, D)) for j in range(2)]))
        staged = [16 * sum(len(q[3]) for q in pieces[n % STAGES:n + 1:STAGES]) for n in range(len(pieces))]
        pieces_of = {l: [n for n, piece in enumerate(pieces) if piece[0] == l] for l in range(NL)}

        def stage(n, ncols):
            half = (QS, KS)[n % STAGES // 2][2][:, :, :, :].rearrange("p h c t -> p (h c t)").bitcast(F32)
            return half[:, n % 2 * C * 2 * D:][:, 0:C * ncols].rearrange("p (c n) -> p c n", c=C)

        def stack_rest(eng, l):
            eng.memset(QS[l][ROWS:P, :, :, :], 0.0)
            return eng.memset(KS[l][ROWS:P, :, :, :], 1.0)

        block = stack.enter_context(nc.Block())

        @block.sync
        def _(sp):
            n_const = 0
            for dst, src in ((CONST[:, :], consts), (MI[:, :], mask), (RB[:, :], rows),
                             (COLB[:, :, :, :].rearrange("p l q c -> p (l q c)"), cols),
                             (EB[:, :], eb)):
                sp.dma_start(dst, src).then_inc(const_loaded, 16)
                n_const += 16
            sp.dma_start(X[0][:, :, :], x_v[0]).then_inc(x_loaded, 16)
            sp.dma_start(CTX[:, :, :], ctx_v[0]).then_inc(ctx_loaded, 16)

            def load_piece(n):
                _, _, ncols, parts = pieces[n]
                if n >= STAGES:
                    sp.wait_ge(w_lo_done, n - STAGES + 1)
                for off, src in parts:
                    sp.dma_start(stage(n, ncols)[:, :, off:off + src.shape[2]], src).then_inc(stage_loaded[n % STAGES], 16)

            for n in range(STAGES):
                load_piece(n)

            def prepare(l):
                for n in range(STAGES * l, min(STAGES * (l + 1), len(pieces))):
                    if l:
                        load_piece(n)

            def step(at, i, max_base, att_base, proj_base):
                def value(v):
                    if i is None:
                        sp.compute_val(v)
                    return v

                turns = {l: value(proj_base + proj_turn(l, i)) for l, lag in PROJ_ORDER if active(i, lag)}
                all_stored = {l: value((proj_base + proj_turn(l, i)) * (16 * PARTS)) for l in turns}
                all_stacked = {c: value(at[c] * (16 * PARTS)) for c in at}

                def store_part(x, l, k):
                    done = (hi_done, mid_done, low_done)[k]
                    m, val = before(PROJ_ORDER, l, {c: c for c in at}, i)
                    if k == 0 and m is not None:
                        sp.wait_ge(stacked[(x, m)], all_stacked[val])
                    sp.wait_ge(done[x], turns[l])
                    sp.dma_start(split[x][:, PLACE[x][k], :, :],
                                 (QP if x == "q" else KP)[:, k, :, :].rearrange("p c t -> p (c t)")
                                 ).then_inc(stored[x], 16)

                def load_stack(x, l, lag):
                    dst, row = (QS if x == "q" else KS)[l], 0
                    sp.wait_ge(stored[x], all_stored[l])
                    if i is None or i > lag:
                        sp.wait_ge(z_psum[(l, 1)], at[-lag])
                    for a, b in STACK_FROM[x]:
                        end = row + (b - a) * DH
                        sp.dma_start(dst[row:end, :, :, :].rearrange("r h c t -> r h (c t)"),
                                     split[x][:, a:b, :, :].rearrange("h s r t -> h (s r) t").rearrange("h q t -> q h t")).then_inc(stacked[(x, l)], 16)
                        row = end

                for kind, l, lag, part in UNITS:
                    if not active(i, lag):
                        continue
                    new = at[1 - lag]
                    if kind == "q":
                        store_part("q", l, 0)
                    if kind == "k":
                        store_part("k", l, 0)
                    if kind in ("qmid", "kmid"):
                        store_part(kind[0], l, 1)
                        store_part(kind[0], l, 2)
                    if kind == "stack":
                        load_stack("q", l, lag)
                        load_stack("k", l, lag)
                    if kind == "stack" and l == 0 and (i is None or i < NSTEP - 1):
                        sp.wait_ge(xt_psum[0], new)
                        sp.wait_ge(xb_done[0], new)
                        sp.dma_start(X[0][:, :, :], x_v[new]).then_inc(x_loaded, 16)
                    if kind == "q" and l == 1 and (i is None or i - lag < NSTEP - 1):
                        sp.wait_ge(ct_psum, new)
                        sp.dma_start(CTX[:, :, :], ctx_v[new]).then_inc(ctx_loaded, 16)
                    if kind == "maxload":
                        sp.wait_ge(mt_done[l], new)
                        for k in range(MAX_PARTS):
                            sp.dma_start(QS[l][ROWS + k:ROWS + k + 1, :, :, :].rearrange("o h c t -> o (h c) t"),
                                         MT[l][k * H:(k + 1) * H, :]).then_inc(max_stacked[l], 16)
                    if kind == "store":
                        sp.wait_ge(norm_done[2], new)
                        sp.dma_start(out_v[at[-lag]], XB[2][:, :, :]).then_inc(out_stored, 16)

            steps(sp, step, NSTEP - 1, prepare)
            sp.wait_ge(out_stored, 16 * NSTEP)
            sp.wait_ge(const_loaded, n_const)
            for x in "qk":
                sp.wait_ge(stored[x], 16 * PARTS * NL * NSTEP)

        CONSTS_LOADED = 16 * 5

        @block.tensor
        def _(pe):
            pe.wait_ge(setup_v, 1)
            for j in range(2):
                pe.transpose(WB[j][:, 0:P // 2].bitcast(BF16), MQ[j][:, :], IDB[:, :]).then_inc(setup_pe, 1)
            pe.wait_ge(setup_v, 3)
            pe.wait_ge(setup_p, 2)

            def prepare(l):
                pe.wait_ge(w_lo_done, pieces_of[l][-1] + 1)
                if l == 2:
                    pe.wait_ge(setup_v, 4)


            def three_pass(dst, lhs_h, lhs_l, rhs_h, rhs_l):
                for c in range(C):
                    mm = None
                    for k, (a, b) in enumerate(((lhs_h, rhs_h), (lhs_h, rhs_l), (lhs_l, rhs_h))):
                        mm = pe.matmul(dst, a(c), b(c), start=(c == 0 and k == 0), stop=(c == C - 1 and k == 2))
                return mm

            def transpose_tokens(src, dst):
                for b in range(PB):
                    for c in range(C):
                        mm = pe.transpose(dst[:, c * TOK + b * P:c * TOK + (b + 1) * P],
                                          src[:, b, c * P:(c + 1) * P], IDF[:, :])
                return mm

            def step(at, i, max_base, att_base, proj_base):
                def mine(name, l):
                    claim(pe, name, l, at, i)
                    return bank(name, l)

                def xt(l, new, part):
                    if l == 0:
                        pe.wait_ge(x_loaded, new * 16)
                    else:
                        pe.wait_ge(norm_done[l - 1], new)
                    transpose_tokens(X[l], mine("xt", l)).then_inc(xt_psum[l], 1)

                def ct(l, new, part):
                    pe.wait_ge(ctx_loaded, new * 16)
                    transpose_tokens(CTX, mine("ct", 1)).then_inc(ct_psum, 1)

                def feature_major(name, l, off, hi, lo, done):
                    dst = mine(name, l)
                    for t in range(C):
                        mm = three_pass(dst[:, t * TOK:(t + 1) * TOK],
                                        lambda c: WH[l][:, c, off + t * P:off + (t + 1) * P],
                                        lambda c: WL[l][:, c, off + t * P:off + (t + 1) * P],
                                        lambda c: hi[:, c, :], lambda c: lo[:, c, :])
                    mm.then_inc(done, 1)

                def q(l, new, part):
                    pe.wait_ge(xl_done[l], new)
                    feature_major("q", l, WQ, XH[l], XL[l], q_psum[l])

                def source(l):
                    return (CH, CL) if l == 1 else (XH[l], XL[l])

                def k(l, new, part):
                    if l == 1:
                        pe.wait_ge(cl_done, new)
                    feature_major("k", l, WK, *source(l), k_psum[l])

                def v(l, new, part):
                    hi, lo = source(l)
                    width = VG if l == 2 else D
                    for b in range(PB):
                        if l == 2:
                            dst, done = mine(("v", "v1")[b], l)[:, 0:width], v_psum[(l, b)]
                        else:
                            dst, done = (mine("v", l) if b == 0 else bank("v", l))[:, b * D:(b + 1) * D], v_psum[(l, 0)]
                        mm = three_pass(dst, lambda c: hi[:, c, b * P:(b + 1) * P], lambda c: lo[:, c, b * P:(b + 1) * P],
                                        lambda c: WH[l][:, c, WV:WV + width], lambda c: WL[l][:, c, WV:WV + width])
                        if l == 2 or b == 1:
                            mm.then_inc(done, 1)

                def head(stack, l, h, b, rows=ROWS):
                    return stack[l][0:rows, h % HC, h // HC, b * P:(b + 1) * P]

                def row_max(l, new, p):
                    if p == 0:
                        for x in "qk":
                            pe.wait_ge(stacked[(x, l)], new * 16 * PARTS)
                    g = turn(MAX_ORDER, l, p, i)
                    if i != 0 or g >= 2:
                        pe.wait_ge(max_read, max_base + (g - 1))
                    dst = SM[g % 2]
                    for b in range(PB):
                        for h2 in range(2):
                            mm = pe.matmul(dst[:, b, h2, :], head(QS, l, 2 * p + h2, b), head(KS, l, 2 * p + h2, b),
                                           start=(b + h2 == 0), stop=(b + h2 == 2 and l == 2), skip_group_check=True)
                    if l < 2:
                        mm = pe.matmul(dst[:, :, :, :], IDB[:, :],
                                       MQ[l][:, :].unsqueeze(1).to_broadcast([P, 2 * PB, P]),
                                       start=False, stop=True, skip_group_check=True)
                    mm.then_inc(max_psum, 1)

                def max_t(l, new, part):
                    pe.wait_ge(nm_done[l], new)
                    dst = mine("maxt", l)
                    for b in range(PB):
                        mm = pe.transpose(dst[0:MAX_PARTS * H, b * P // 2:(b + 1) * P // 2].bitcast(BF16),
                                          NMB[:, b, :, :, :].rearrange("p k h c -> p (k h c)"), IDB[:, :])
                    mm.then_inc(mt_psum[l], 1)

                def scores(l, p):
                    g = turn(ATT_ORDER, l, p, i)
                    if i != 0 or g >= 2:
                        pe.wait_ge(probs_done, att_base + (g - 1))
                    dst = SS[g % 2]
                    rows = P
                    for b in range(PB):
                        for h2 in range(2):
                            mm = pe.matmul(dst[:, b, h2, :], head(KS, l, 2 * p + h2, b, rows),
                                           head(QS, l, 2 * p + h2, b, rows), start=(b + h2 == 0),
                                           stop=(b + h2 == 2 and l == 2), skip_group_check=True)
                    if l < 2:
                        mm = pe.matmul(dst[:, :, :, :], IDB[:, :],
                                       MK[l][:, :].unsqueeze(1).to_broadcast([P, 2 * PB, P]),
                                       start=False, stop=True, skip_group_check=True)
                    mm.then_inc(score_psum, 1)

                def values(l, p):
                    g = turn(ATT_ORDER, l, p, i)
                    dst = mine(f"pv{p // 4}", l) if p % 4 == 0 else bank(f"pv{p // 4}", l)
                    pe.wait_ge(probs_done, att_base + (g + 1))
                    for b in range(PB):
                        for h2 in range(2):
                            j = QUAD * (2 * b + h2)
                            mm = pe.matmul(dst[j:j + QUAD, (p % 4) * P:(p % 4 + 1) * P], VA[l][:, b, 2 * p + h2, :],
                                           PR[slot(ATT_ORDER, l, p, i, 3)][:, b, h2, :],
                                           start=True, stop=True, tile_position=(0, j))
                    mm.then_inc(pv_psum, 1)

                def attend(l, new, p):
                    if p == 0:
                        pe.wait_ge(max_stacked[l], new * 16 * MAX_PARTS)
                        for b in range(PB if l == 2 else 1):
                            pe.wait_ge(v_done[(l, b)], new)
                    if p < PAIRS:
                        scores(l, p)
                    if p > 0:
                        values(l, p - 1)

                def z_tokens(l, new, f):
                    pe.wait_ge(za_done[(l, f)], new)
                    dst = mine(f"z{f}", l)
                    for p in range(4):
                        mm = pe.transpose(dst[:, p * P:(p + 1) * P], ZA[f][:, p, :], IDF[:, :])
                    mm.then_inc(z_psum[(l, f)], 1)

                def z_transposed(l, new, part):
                    for f in range(2):
                        pe.wait_ge(z_done[(l, f)], new)
                    transpose_tokens(Z[0][:, :, :, :].rearrange("p b h d -> p b (h d)"),
                                     mine("zt", l)).then_inc(zt_psum[l], 1)

                def out_proj(l, new, part):
                    pe.wait_ge(zl_done[l], new)
                    dst = mine("out", l)
                    for b in range(PB):
                        mm = three_pass(dst[:, b * D:(b + 1) * D],
                                        lambda c: ZH[:, c, b * P:(b + 1) * P], lambda c: ZL[:, c, b * P:(b + 1) * P],
                                        lambda c: WH[l][:, c, WO:WO + D], lambda c: WL[l][:, c, WO:WO + D])
                    mm.then_inc(o_psum[l], 1)

                def gate_t(l, new, part):
                    pe.wait_ge(combine_done, new)
                    dst = mine("gate", 2)
                    for b in range(PB):
                        mm = pe.transpose(dst[0:QUAD, b * P:(b + 1) * P], CB[:, b, :], IDF[:, :])
                    mm.then_inc(gt_psum, 1)

                def expert_bias(l, new, part):
                    pe.wait_ge(gt_done, new)
                    dst = mine("bias", 2)
                    for b in range(PB):
                        mm = pe.matmul(dst[:, b * D:(b + 1) * D], CBT[0:E, b * P:(b + 1) * P], EB[:, :],
                                       start=True, stop=True)
                    mm.then_inc(eb_psum, 1)

                def experts(l, new, g):
                    b, o = g % PB, WE + (g // PB) * 2 * D
                    three_pass(mine(f"e{g}", 2)[:, :],
                               lambda c: XH[2][:, c, b * P:(b + 1) * P], lambda c: XL[2][:, c, b * P:(b + 1) * P],
                               lambda c: WH[2][:, c, o:o + 2 * D],
                               lambda c: WL[2][:, c, o:o + 2 * D]).then_inc(e_psum[g], 1)

                work = {"xt": xt, "ct": ct, "q": q, "k": k, "v": v, "max": row_max, "maxt": max_t,
                        "attend": attend, "z": z_tokens, "zt": z_transposed, "out": out_proj, "gate": gate_t,
                        "experts": experts, "bias": expert_bias}
                for kind, l, lag, part in UNITS:
                    if kind in work and active(i, lag):
                        work[kind](l, at[1 - lag], part)

            steps(pe, step, prepare=prepare)

        @block.scalar
        def _(act):
            act.wait_ge(setup_v, 3)

            def prepare(l):
                for n in pieces_of[l]:
                    _, c0, ncols, _ = pieces[n]
                    act.wait_ge(stage_loaded[n % STAGES], staged[n])
                    act.activation(WH[l][:, :, c0:c0 + ncols], stage(n, ncols), ACT.Copy).then_inc(w_hi_done, 1)

            def step(at, i, max_base, att_base, proj_base):
                def rounded(dst, src, ready, new, done):
                    act.wait_ge(ready, new)
                    act.activation(dst[:, :, :].rearrange("p c t -> p (c t)"), src[:, :], ACT.Copy).then_inc(done, 1)

                def xt(l, new, part):
                    rounded(XH[l], bank("xt", l), xt_psum[l], new, xh_done[l])

                def ct(l, new, part):
                    rounded(CH, bank("ct", 1), ct_psum, new, ch_done)

                def project(x, l):
                    n = proj_base + proj_turn(l, i)
                    full, parts, src = (QF, QP, bank("q", l)) if x == "q" else (KF, KP, bank("k", l))
                    if not (isinstance(n, int) and n == 1):
                        act.wait_ge(low_done[x], n - 1)
                    for t in range(C):
                        if x == "q":
                            ins = act.activation(full[:, t, :], src[:, t * TOK:(t + 1) * TOK], ACT.Identity,
                                                 bias=QBI[:, l, t:t + 1], scale=SCALE)
                        else:
                            ins = act.activation(full[:, t, :], src[:, t * TOK:(t + 1) * TOK], ACT.Identity,
                                                 bias=COLB[:, l, 1, t:t + 1])
                    return n, full, parts, ins

                def high(x, n, full, parts):
                    if not (isinstance(n, int) and n == 1):
                        act.wait_ge(stored[x], (n - 1) * 16 * PARTS)
                    act.activation(parts[:, 0, :, :], full[:, :, :], ACT.Copy).then_inc(hi_done[x], 1)

                def middle(x, l):
                    n = proj_base + proj_turn(l, i)
                    full, parts = (QF, QP) if x == "q" else (KF, KP)
                    act.wait_ge(rest_done[x], n)
                    act.activation(parts[:, 1, :, :], full[:, :, :], ACT.Copy).then_inc(mid_done[x], 1)

                def q(l, new, part):
                    act.wait_ge(q_psum[l], new)
                    n, full, parts, ins = project("q", l)
                    ins.then_inc(qf_done[l], 1)
                    act.wait_ge(qf_done[l], new)
                    high("q", n, full, parts)

                def k(l, new, part):
                    act.wait_ge(k_psum[l], new)
                    n, full, parts, ins = project("k", l)
                    ins.then_inc(kf_done[l], 1)
                    act.wait_ge(kf_done[l], new)
                    high("k", n, full, parts)

                def q_middle(l, new, part):
                    middle("q", l)

                def k_middle(l, new, part):
                    middle("k", l)

                def gate_exps(l, new, part):
                    act.wait_ge(gate_max, new)
                    for b in range(PB):
                        ins = act.activation(GE[:, b, :], GL[:, b, :], ACT.Exp, bias=GN[:, b:b + 1],
                                             accum_out=GS[:, b:b + 1])
                    ins.then_inc(gate_exp, 1)

                def max_t(l, new, part):
                    act.wait_ge(mt_psum[l], new)
                    act.activation(MT[l][:, :], bank("maxt", l)[0:MAX_PARTS * H, 0:P].bitcast(BF16), ACT.Copy).then_inc(mt_done[l], 1)

                def z_half(l, f):
                    act.wait_ge(pv_psum, att_base + (turn(ATT_ORDER, l, 4 * f + 3, i) + 1))
                    act.activation(ZA[f][:, :, :].rearrange("p k q -> p (k q)"), bank(f"pv{f}", l)[:, :],
                                   ACT.Copy).then_inc(za_done[(l, f)], 1)

                def attend(l, new, p):
                    if p in (5, 8):
                        z_half(l, p // 8)
                    if p == PAIRS:
                        return
                    g = turn(ATT_ORDER, l, p, i)
                    act.wait_ge(score_psum, att_base + (g + 1))
                    if i != 0 or g >= 3:
                        act.wait_ge(pv_psum, att_base + (g - 2))
                    act.activation(PR[slot(ATT_ORDER, l, p, i, 3)][:, :, :, :], SS[g % 2][:, :, :, :],
                                   ACT.Exp).then_inc(probs_done, 1)

                def z_transposed(l, new, part):
                    rounded(ZH, bank("zt", l), zt_psum[l], new, zh_done[l])

                work = {"xt": xt, "ct": ct, "q": q, "k": k, "qmid": q_middle, "kmid": k_middle, "gexp": gate_exps,
                        "maxt": max_t, "attend": attend, "zt": z_transposed}
                for kind, l, lag, part in UNITS:
                    if kind in work and active(i, lag):
                        work[kind](l, at[1 - lag], part)

            steps(act, step, prepare=prepare)

        @block.vector
        def _(dve):
            own = [0]

            def setup_link(ins):
                own[0] += 1
                ins.then_inc(dve_setup, 1)
                dve.wait_ge(dve_setup, own[0])

            dve.wait_ge(const_loaded, CONSTS_LOADED)
            dve.tensor_copy(IDB[:, :], CONST[:, 0:P])
            dve.tensor_scalar(MQ[0][:, :], CONST[:, P:2 * P], -MASKED, MASKED, ALU.mult, ALU.add)
            setup_link(dve.tensor_copy(MF[:, :], MI[:, :]))
            setup_link(dve.tensor_scalar(MQ[1][:, :], MF[:, :], 0.0, MASKED, ALU.is_equal, ALU.mult))
            setup_link(dve.tensor_scalar(QBI[:, :, :], COLB[:, :, 0, :], SCALE, None, ALU.mult))
            dve.memset(NHALF[:, :], -0.5)
            dve.memset(EPSC[:, :], EPS)
            setup_link(dve.memset(CB[:, :, :], 0.0))
            dve.memset(GN[:, :], 0.0).then_inc(setup_v, 1)
            for j in range(2):
                dve.wait_ge(setup_pe, j + 1)
                dve.tensor_copy(MK[j][:, :], WB[j][:, 0:P // 2].bitcast(BF16)).then_inc(setup_v, 1)

            def prepare(l):
                for n in pieces_of[l]:
                    _, c0, ncols, _ = pieces[n]
                    dve.wait_ge(w_hi_done, n + 1)
                    dve.tensor_tensor(WL[l][:, :, c0:c0 + ncols], stage(n, ncols),
                                      WH[l][:, :, c0:c0 + ncols].bitcast(F32), ALU.subtract).then_inc(w_lo_done, 1)
                if l == 0:
                    dve.wait_ge(setup_p, 2)
                if l == 2:
                    dve.wait_ge(w_lo_done, len(pieces))
                    stack_rest(dve, 2).then_inc(setup_v, 1)

            IOTA = CONST[:, 2 * P:2 * P + E]

            def step(at, i, max_base, att_base, proj_base):
                def carry(s, value):
                    dve.wait_ge(s, value)
                    dve.memset(SPARE[:, :], 0.0)

                per = sum(links(kind, l, part) for kind, l, _, part in UNITS)
                linked = [link_base(i) if i is not None else dve.snap(at[0] * per - (per * (DEPTH + 1) - link_base(DEPTH + 1))), 0]

                def link(ins, carried=False):
                    linked[1] += 1
                    ins.then_inc(vector_link, 1)
                    if carried:
                        carry(vector_link, linked[0] + linked[1])
                    else:
                        dve.wait_ge(vector_link, linked[0] + linked[1])

                def flat(t):
                    return t[:, :, :].rearrange("p c t -> p (c t)")

                def low(dst, src, hi, ready, new, done):
                    dve.wait_ge(ready, new)
                    dve.tensor_tensor(flat(dst), src[:, :], flat(hi).bitcast(F32), ALU.subtract).then_inc(done, 1)

                def xt(l, new, part):
                    low(XL[l], bank("xt", l), XH[l], xh_done[l], new, xl_done[l])

                def ct(l, new, part):
                    low(CL, bank("ct", 1), CH, ch_done, new, cl_done)

                def v(l, new, part):
                    for b in range(PB):
                        if l == 2:
                            dve.wait_ge(v_psum[(l, b)], new)
                            src = bank(("v", "v1")[b], l)
                            dve.tensor_tensor(GL[:, b, :], src[:, D:VG], RB[:, RB_V[2] + D:RB_V[2] + VG], ALU.add)
                            o = 0
                        else:
                            if b == 0:
                                dve.wait_ge(v_psum[(l, 0)], new)
                            src = bank("v", l)
                            o = b * D
                        ins = dve.tensor_tensor(VA[l][:, b, :, 0:DH],
                                                src[:, o:o + D].rearrange("p (h d) -> p h d", h=H),
                                                RB[:, RB_V[l]:RB_V[l] + D].rearrange("p (h d) -> p h d", h=H), ALU.add)
                        if l == 2:
                            ins.then_inc(v_done[(l, b)], 1)
                    if l < 2:
                        ins.then_inc(v_done[(l, 0)], 1)
                    else:
                        dve.wait_ge(v_done[(2, 1)], new)
                        dve.tensor_reduce(GN[:, :], GL[:, :, :], AX.X, ALU.max, negate=True).then_inc(gate_max, 1)

                def gate_top(n):
                    dve.wait_ge(gate_exp, n)
                    link(dve.reciprocal(GR[:, :], GS[:, :]))
                    for b in range(PB):
                        ins = dve.tensor_scalar(GP[:, b, :], GE[:, b, :], GR[:, b:b + 1], None, ALU.mult)
                    link(ins, carried=True)
                    for b in range(PB):
                        ins = dve.max(GT[:, b, :], GP[:, b, :])
                    link(ins, carried=True)
                    for b in range(PB):
                        ins = dve.max_index(GI[:, b, :], GT[:, b, :], GP[:, b, :])
                    link(ins)
                    link(dve.tensor_copy(GF[:, :, :], GI[:, :, :]))
                    for b in range(PB):
                        dve.tensor_scalar(G1[:, b, :], IOTA, GF[:, b, 0:1], GT[:, b, 0:1], ALU.is_equal, ALU.mult)
                        ins = dve.tensor_scalar(G2[:, b, :], IOTA, GF[:, b, 1:2], GT[:, b, 1:2], ALU.is_equal,
                                                ALU.mult)
                    link(ins)
                    dve.tensor_tensor(CB[:, :, 0:E], G1[:, :, :], G2[:, :, :], ALU.add).then_inc(combine_done, 1)

                def row_max(l, new, p):
                    g = turn(MAX_ORDER, l, p, i)
                    dve.wait_ge(max_psum, max_base + (g + 1))
                    dve.tensor_reduce(NM[:, :, 2 * p:2 * p + 2], SM[g % 2][:, :, :, :], AX.X, ALU.max,
                                      negate=True).then_inc(max_read, 1)
                    if l == 2 and p == 1:
                        gate_top(new)
                    if p < PAIRS - 1:
                        return
                    m, val = before(MAX_ORDER, l, at, i)
                    if m is not None:
                        dve.wait_ge(mt_psum[m], val)
                    dve.wait_ge(max_read, max_base + (g + 1))
                    maxima = NM[:, :, :].rearrange("p b (c h) -> p b h c", c=C)
                    link(dve.tensor_copy(NMB[:, :, 0, :, :], maxima))
                    ins = dve.tensor_tensor(NMB[:, :, 1, :, :], maxima, NMB[:, :, 0, :, :], ALU.subtract)
                    ins.then_inc(nm_done[l], 1)

                def z_tokens(l, new, f):
                    dve.wait_ge(z_psum[(l, f)], new)
                    src = bank(f"z{f}", l)[:, :].rearrange("q (p b h d) -> q p b h d", p=4, b=PB, h=2)
                    rz = RZ[:, :, 4 * f:4 * f + 4, :]
                    for b in range(PB):
                        ins = dve.reciprocal(rz[:, b, :, :].unsqueeze(3), src[:, :, b, :, DH:DH + 1])
                    link(ins)
                    for b in range(PB):
                        ins = dve.tensor_tensor(Z[l // 2][:, b, 8 * f:8 * f + 8, :].rearrange("q (p h) d -> q p h d", p=4),
                                                src[:, :, b, :, 0:DH],
                                                rz[:, b, :, :].unsqueeze(3).to_broadcast([P, 4, 2, DH]), ALU.mult)
                    ins.then_inc(z_done[(l, f)], 1)

                def z_transposed(l, new, part):
                    low(ZL, bank("zt", l), ZH, zh_done[l], new, zl_done[l])

                def statistics(l, new):
                    for b in range(PB):
                        ins = dve.bn_stats(ST[:, l, b, :], XB[l][:, b, :])
                    link(ins, carried=True)
                    for b in range(PB):
                        ins = dve.bn_aggr(MV[:, l, b, :], ST[:, l, b, :])
                    ins.then_inc(mv_done[l], 1)

                def normalise(l, new, lag):
                    old = at[-lag]
                    dst = X[l + 1] if l < 2 else XB[2]
                    if l < 2 and (i is None or i > lag):
                        dve.wait_ge(xb_done[1] if l == 0 else eb_done, old)
                        dve.wait_ge(xt_psum[l + 1], old)
                    dve.wait_ge(rs_done[l], new)
                    for b in range(PB):
                        ins = dve.tensor_scalar(dst[:, b, :], XB[l][:, b, :], MV[:, l, b, 0:1], RS[:, l, b:b + 1],
                                                ALU.subtract, ALU.mult)
                    ins.then_inc(norm_done[l], 1)

                def out_proj(l, new, part):
                    dve.wait_ge(o_psum[l], new)
                    dve.wait_ge(xb_done[l], new)
                    xb = XB[l][:, :, :].rearrange("p b d -> p (b d)")
                    dve.tensor_tensor(xb, bank("out", l)[:, :], xb, ALU.add).then_inc(sum_done[l], 1)
                    dve.wait_ge(sum_done[l], new)
                    statistics(l, new)

                def gate_t(l, new, part):
                    dve.wait_ge(gt_psum, new)
                    dve.tensor_copy(CBT[:, :], bank("gate", 2)[0:QUAD, 0:TOK]).then_inc(gt_done, 1)

                def expert_bias(l, new, lag):
                    if i is None or i > lag:
                        dve.wait_ge(out_stored, at[-lag] * 16)
                    dve.wait_ge(eb_psum, new)
                    dve.tensor_tensor(XB[2][:, :, :].rearrange("p b d -> p (b d)"), bank("bias", 2)[:, :],
                                      X[2][:, :, :].rearrange("p b d -> p (b d)"), ALU.add).then_inc(eb_done, 1)

                def experts(l, new, g):
                    b, acc = g % PB, XB[2]
                    dve.wait_ge(e_psum[g], new)
                    for half in range(2):
                        e = 2 * (g // PB) + half
                        if half:
                            dve.wait_ge(e_half[g], new)
                        elif g < PB:
                            dve.wait_ge(eb_done, new)
                        else:
                            dve.wait_ge(e_done[g - PB], new)
                        dve.scalar_tensor_tensor(
                            out=acc[:, b, :], in0=bank(f"e{g}", 2)[:, half * D:(half + 1) * D],
                            scalar=CB[:, b, e:e + 1], in1=acc[:, b, :], op0=ALU.mult,
                            op1=ALU.add).then_inc((e_done if half else e_half)[g], 1)

                def finish(l, new, part):
                    for g in range(E - PB, E):
                        dve.wait_ge(e_done[g], new)
                    for f in range(2):
                        dve.wait_ge(z_done[(2, f)], new)
                    dve.tensor_tensor(XB[2][:, :, :], XB[2][:, :, :],
                                      Z[1][:, :, :, :].rearrange("p b h d -> p b (h d)"),
                                      ALU.add).then_inc(sum_done[2], 1)
                    dve.wait_ge(sum_done[2], new)
                    statistics(2, new)

                work = {"xt": xt, "ct": ct, "v": v, "max": row_max, "z": z_tokens,
                        "zt": z_transposed, "out": out_proj, "gate": gate_t, "experts": experts, "finish": finish,
                        "bias": expert_bias, "norm": normalise}
                for kind, l, lag, part in UNITS:
                    if kind in work and active(i, lag):
                        work[kind](l, at[1 - lag], lag if kind in ("norm", "bias") else part)

            steps(dve, step, prepare=prepare)

        @block.gpsimd
        def _(pool):
            for l in range(NL):
                ins = pool.memset(VA[l][:, :, :, DH:QUAD], 1.0)
            ins.then_inc(setup_p, 1)
            pool.wait_ge(setup_p, 1)
            for l in (0, 1):
                ins = stack_rest(pool, l)
            ins.then_inc(setup_p, 1)
            pool.wait_ge(setup_p, 2)
            pool.wait_ge(setup_v, 1)

            def step(at, i, max_base, att_base, proj_base):
                def residual(l, lag):
                    new = at[1 - lag]
                    if l == 0:
                        pool.wait_ge(x_loaded, new * 16)
                    else:
                        pool.wait_ge(norm_done[l - 1], new)
                    if i is None or i > lag:
                        pool.wait_ge(norm_done[l], at[-lag])
                    for b in range(PB):
                        ins = pool.tensor_tensor(XB[l][:, b, :], X[l][:, b, :], RB[:, RB_O[l]:RB_O[l] + D], ALU.add)
                    ins.then_inc(xb_done[l], 1)

                def rstd(l, lag):
                    new = at[1 - lag]
                    pool.wait_ge(mv_done[l], new)
                    pool.tensor_tensor(VE[:, l, :], MV[:, l, :, 1], EPSC[:, :], ALU.add).then_inc(ve_done[l], 1)
                    pool.wait_ge(ve_done[l], new)
                    pool.tensor_tensor(RS[:, l, :], VE[:, l, :], NHALF[:, :], ALU.pow).then_inc(rs_done[l], 1)

                def rest(x, l):
                    n = proj_base + proj_turn(l, i)
                    full, parts = (QF, QP) if x == "q" else (KF, KP)
                    pool.wait_ge(hi_done[x], n)
                    pool.tensor_tensor(full[:, :, :], full[:, :, :], parts[:, 0, :, :], ALU.subtract).then_inc(rest_done[x], 1)

                def lowest(x, l):
                    n = proj_base + proj_turn(l, i)
                    full, parts = (QF, QP) if x == "q" else (KF, KP)
                    pool.wait_ge(mid_done[x], n)
                    pool.tensor_tensor(parts[:, 2, :, :], full[:, :, :], parts[:, 1, :, :], ALU.subtract).then_inc(low_done[x], 1)

                for kind, l, lag, part in UNITS:
                    if active(i, lag):
                        if kind == "q":
                            rest("q", l)
                        if kind == "k":
                            rest("k", l)
                        if kind in ("qmid", "kmid"):
                            lowest(kind[0], l)
                        if kind == "v" and l < 2:
                            residual(l, lag)
                        if kind == "norm":
                            rstd(l, lag)

            steps(pool, step)


def kernel(x, ctx_1024, mask_1x1xSxS2_ik0, L0_attn_W_qkv, L0_attn_b_qkv, L0_attn_W_proj, L0_attn_b_proj,
           L0_xattn_wq, L0_xattn_bq, L0_xattn_wk, L0_xattn_bk, L0_xattn_wv, L0_xattn_bv, L0_xattn_wo, L0_xattn_bo,
           L0_ffn_W_qkv, L0_ffn_b_qkv, L0_ffn_W_gate, L0_ffn_b_gate, L0_ffn_W_experts, L0_ffn_b_experts):
    import numpy as np
    import concourse.bacc as bacc
    from concourse.bass_utils import run_bass_kernel_spmd

    def a(v):
        return np.asarray(v)

    consts = np.concatenate([
        np.eye(P), np.tril(np.ones((P, P))),
        np.tile(np.arange(E), (P, 1)),
    ], axis=1).astype(np.float32)
    row = np.concatenate([a(L0_attn_b_qkv)[2 * D:], a(L0_attn_b_proj), a(L0_xattn_bv), a(L0_xattn_bo),
                          a(L0_ffn_b_qkv)[2 * D:], a(L0_ffn_b_gate)])
    rows = np.ascontiguousarray(np.broadcast_to(row[None, :], (P, RB_COLS)))
    col = np.stack([a(L0_attn_b_qkv)[:2 * D], np.concatenate([a(L0_xattn_bq), a(L0_xattn_bk)]),
                    a(L0_ffn_b_qkv)[:2 * D]])
    cols = np.ascontiguousarray(col.reshape(NL * 2 * C, P).T)
    arrays = {
        "x": a(x), "ctx": a(ctx_1024), "mask": np.ascontiguousarray(a(mask_1x1xSxS2_ik0).reshape(P, P)),
        "qkv0": a(L0_attn_W_qkv), "o0": a(L0_attn_W_proj),
        "q1": np.ascontiguousarray(a(L0_xattn_wq).T), "k1": np.ascontiguousarray(a(L0_xattn_wk).T),
        "v1": np.ascontiguousarray(a(L0_xattn_wv).T), "o1": np.ascontiguousarray(a(L0_xattn_wo).T),
        "qkv2": a(L0_ffn_W_qkv), "gate": a(L0_ffn_W_gate), "experts": a(L0_ffn_W_experts),
        "eb": a(L0_ffn_b_experts), "rows": rows, "cols": cols, "consts": consts,
    }
    nc = bacc.Bacc("TRN2", target_bir_lowering=False, num_devices=1)
    t = {n: nc.dram_tensor(f"in_{n}", v.shape, mybir.dt.from_np(v.dtype), kind="ExternalInput").ap()
         for n, v in arrays.items()}
    out = nc.dram_tensor("out_0", (B, P, D), F32, kind="ExternalOutput").ap()
    split = {x: nc.dram_tensor(f"{x}_split", (HC, PARTS, DH, C * TOK), BF16, kind="Internal").ap() for x in "qk"}
    decoder(nc, t["x"], t["ctx"], t["mask"], t, t["rows"], t["cols"], t["eb"], t["consts"], split, out)
    r = run_bass_kernel_spmd(nc, [{f"in_{n}": v for n, v in arrays.items()}], core_ids=[0])
    return r.results[0]["out_0"]
```
